# Optimizing a Trainium2 kernel written in Bass

```python
import numpy as np
import jax
import jax.numpy as jnp

def _softmax(x, axis=-1):
    return jax.nn.softmax(x, axis=axis)

def _gelu(x):
    return jax.nn.gelu(x, approximate=True)

def _silu(x):
    return jax.nn.silu(x)

def _sigmoid(x):
    return jax.nn.sigmoid(x)

def _layernorm(x, axis=-1, eps=1e-05):
    m = jnp.mean(x, axis=axis, keepdims=True)
    v = jnp.var(x, axis=axis, keepdims=True)
    return (x - m) / jnp.sqrt(v + eps)

def _scatter_add(tgt, idx, src, axis=0):
    return tgt.at[idx].add(src)

def _segment_sum(src, seg, n):
    return jax.ops.segment_sum(src, seg, n)
kernel_name = 'mk_gnn_preln_d4_gnn_r8_ad2422'

def setup_inputs(seed: int=0):
    np.random.seed(seed)
    _w = jnp.asarray

    def _rec_inputs():
        import jax
        import jax.numpy as jnp
        _gk = jax.random.key(seed)
        x = -0.000202 + 1 * jax.random.normal(jax.random.fold_in(_gk, 1), (6250, 128), jnp.float32)
        src = jax.random.randint(jax.random.fold_in(_gk, 2), (200000,), 0, 6250, jnp.int32)
        dst = jnp.minimum((6250 * jax.random.uniform(jax.random.fold_in(_gk, 3), (200000,)) ** 2.0).astype(jnp.int32), 49999)
        _o = jnp.argsort(dst, stable=True)
        src = src[_o]
        dst = dst[_o]
        edge_attr_128 = 5.93493e-05 + 1.00006 * jax.random.normal(jax.random.fold_in(_gk, 13), (200000, 128), jnp.float32)
        edge_attr_8 = 0.000398945 + 1.00003 * jax.random.normal(jax.random.fold_in(_gk, 14), (200000, 8), jnp.float32)
        return (x, src, dst, edge_attr_128, edge_attr_8)
    x, src, dst, edge_attr_128, edge_attr_8 = _rec_inputs()

    def _L0_gnn_setup():
        import jax, jax.numpy as jnp
        import numpy as np
        N = 6250
        E = 75000
        NODE = 128
        EDGE = 128
        HID = 1024
        G = 50
        IN_DIM = NODE + 3 * EDGE + 1
        key = jax.random.key(seed)
        ks = jax.random.split(key, 8)
        x = jax.random.normal(ks[0], (N, NODE), jnp.float32)
        edge_index = jax.random.randint(ks[1], (2, E), 0, N, dtype=jnp.int64)
        edge_attr = jax.random.normal(ks[2], (E, EDGE), jnp.float32)
        u = jax.random.normal(ks[3], (G, 1), jnp.float32)
        batch = jnp.sort(jax.random.randint(ks[4], (N,), 0, G, dtype=jnp.int64))
        W1 = jax.random.normal(ks[5], (IN_DIM, HID), jnp.float32) / np.sqrt(IN_DIM).astype(np.float32)
        b1 = jnp.zeros((HID,), jnp.float32)
        W2 = jax.random.normal(ks[6], (HID, NODE), jnp.float32) / np.sqrt(HID).astype(np.float32)
        b2 = jnp.zeros((NODE,), jnp.float32)
        return {'x': x, 'edge_index': edge_index, 'edge_attr': edge_attr, 'u': u, 'batch': batch, 'W1': W1, 'b1': b1, 'W2': W2, 'b2': b2}
    _L0_gnn_all = _L0_gnn_setup()
    _L0_gnn_in = {k: v for k, v in _L0_gnn_all.items() if k in ('u', 'W1', 'b1', 'W2', 'b2')}
    del _L0_gnn_all

    def _L1_gnn_setup():
        import jax, jax.numpy as jnp
        import numpy as np
        N_NODES = 6250
        N_EDGES = 100000
        HIDDEN = 128
        N_GRAPHS = 32
        EPS = 1e-05
        key = jax.random.key(seed)
        ks = jax.random.split(key, 8)
        x = jax.random.normal(ks[0], (N_NODES, HIDDEN), dtype=jnp.float32)
        edge_index = jax.random.randint(ks[1], (2, N_EDGES), 0, N_NODES, dtype=jnp.int64)
        batch = jnp.sort(jax.random.randint(ks[2], (N_NODES,), 0, N_GRAPHS, dtype=jnp.int64))
        s = 1.0 / np.sqrt(HIDDEN)
        W_l = jax.random.normal(ks[3], (HIDDEN, HIDDEN), dtype=jnp.float32) * s
        b_l = jnp.zeros((HIDDEN,), dtype=jnp.float32)
        W_r = jax.random.normal(ks[4], (HIDDEN, HIDDEN), dtype=jnp.float32) * s
        gn_weight = jnp.ones((HIDDEN,), dtype=jnp.float32)
        gn_bias = jnp.zeros((HIDDEN,), dtype=jnp.float32)
        gn_mean_scale = jnp.ones((HIDDEN,), dtype=jnp.float32)
        return {'x': x, 'edge_index': edge_index, 'batch': batch, 'W_l': W_l, 'b_l': b_l, 'W_r': W_r, 'gn_weight': gn_weight, 'gn_bias': gn_bias, 'gn_mean_scale': gn_mean_scale}
    _L1_gnn_all = _L1_gnn_setup()
    _L1_gnn_in = {k: v for k, v in _L1_gnn_all.items() if k in ('W_l', 'b_l', 'W_r', 'gn_weight', 'gn_bias', 'gn_mean_scale')}
    del _L1_gnn_all

    def _L2_gnn_setup():
        import jax, jax.numpy as jnp
        import numpy as np
        N_NODES = 12500
        N_EDGES = 200000
        D_IN = 128
        D_OUT = 128
        key = jax.random.key(seed)
        k1, k2, k3, k4 = jax.random.split(key, 4)
        h = jax.random.normal(k1, (N_NODES, D_IN), dtype=jnp.float32)
        src = jax.random.randint(k2, (N_EDGES,), 0, N_NODES, dtype=jnp.int64 if jax.config.jax_enable_x64 else jnp.int32)
        dst = jax.random.randint(k3, (N_EDGES,), 0, N_NODES, dtype=jnp.int64 if jax.config.jax_enable_x64 else jnp.int32)
        W = jax.random.normal(k4, (D_OUT, 2 * D_IN), dtype=jnp.float32) * (1.0 / np.sqrt(2 * D_IN))
        b = jnp.zeros((D_OUT,), dtype=jnp.float32)
        return {'h': h, 'src': src, 'dst': dst, 'W': W, 'b': b}
    _L2_gnn_all = _L2_gnn_setup()
    _L2_gnn_in = {k: v for k, v in _L2_gnn_all.items() if k in ('W', 'b')}
    del _L2_gnn_all

    def _L3_gnn_setup():
        import jax, jax.numpy as jnp
        import numpy as np
        N_NODES = 6250
        N_EDGES = 100000
        IN_F = 128
        OUT_F = 32
        HEADS = 4
        EDGE_DIM = 8
        ALPHA = 0.2
        key = jax.random.key(seed)
        k0, k1, k2, k3, k4 = jax.random.split(key, 5)
        x = jax.random.normal(k0, (N_NODES, IN_F), dtype=jnp.float32)
        edge_index = jax.random.randint(k1, (2, N_EDGES), 0, N_NODES, dtype=jnp.int32)
        edge_attr = jax.random.normal(k2, (N_EDGES, EDGE_DIM), dtype=jnp.float32)
        W = jax.random.normal(k3, (HEADS, IN_F, OUT_F), dtype=jnp.float32) * (1.0 / np.float32(np.sqrt(IN_F)))
        a = jax.random.normal(k4, (HEADS, 2 * OUT_F + EDGE_DIM, 1), dtype=jnp.float32) * np.float32(0.1)
        return {'x': x, 'edge_index': edge_index, 'edge_attr': edge_attr, 'W': W, 'a': a}
    _L3_gnn_all = _L3_gnn_setup()
    _L3_gnn_in = {k: v for k, v in _L3_gnn_all.items() if k in ('W', 'a')}
    del _L3_gnn_all
    return {'x': x, 'src': src, 'dst': dst, 'edge_attr_128': edge_attr_128, 'edge_attr_8': edge_attr_8, 'L0_gnn_u': _L0_gnn_in['u'], 'L0_gnn_W1': _L0_gnn_in['W1'], 'L0_gnn_b1': _L0_gnn_in['b1'], 'L0_gnn_W2': _L0_gnn_in['W2'], 'L0_gnn_b2': _L0_gnn_in['b2'], 'L1_gnn_W_l': _L1_gnn_in['W_l'], 'L1_gnn_b_l': _L1_gnn_in['b_l'], 'L1_gnn_W_r': _L1_gnn_in['W_r'], 'L1_gnn_gn_weight': _L1_gnn_in['gn_weight'], 'L1_gnn_gn_bias': _L1_gnn_in['gn_bias'], 'L1_gnn_gn_mean_scale': _L1_gnn_in['gn_mean_scale'], 'L2_gnn_W': _L2_gnn_in['W'], 'L2_gnn_b': _L2_gnn_in['b'], 'L3_gnn_W': _L3_gnn_in['W'], 'L3_gnn_a': _L3_gnn_in['a']}

def reference(x, src, dst, edge_attr_128, edge_attr_8, L0_gnn_u, L0_gnn_W1, L0_gnn_b1, L0_gnn_W2, L0_gnn_b2, L1_gnn_W_l, L1_gnn_b_l, L1_gnn_W_r, L1_gnn_gn_weight, L1_gnn_gn_bias, L1_gnn_gn_mean_scale, L2_gnn_W, L2_gnn_b, L3_gnn_W, L3_gnn_a):
    import jax
    import jax.numpy as jnp

    def _L0_gnn_ref(x, edge_index, edge_attr, u, batch, W1, b1, W2, b2):
        import jax, jax.numpy as jnp
        import numpy as np
        N = 6250
        E = 75000
        NODE = 128
        EDGE = 128
        HID = 1024
        G = 50
        IN_DIM = NODE + 3 * EDGE + 1
        col = edge_index[1]
        n = x.shape[0]
        seg_sum = jax.ops.segment_sum(edge_attr, col, num_segments=n)
        cnt = jax.ops.segment_sum(jnp.ones((edge_attr.shape[0], 1), edge_attr.dtype), col, num_segments=n)
        seg_max = jax.ops.segment_max(edge_attr, col, num_segments=n)
        has_edges = cnt > 0
        seg_max = jnp.where(has_edges, seg_max, jnp.zeros((), edge_attr.dtype))
        seg_mean = seg_sum / jnp.maximum(cnt, 1.0)
        feats = jnp.concatenate([x, seg_sum, seg_max, seg_mean, u[batch]], axis=1)
        h = jax.nn.gelu(feats @ W1 + b1, approximate=False)
        out = h @ W2 + b2
        return out + x

    def _L1_gnn_ref(x, edge_index, batch, W_l, b_l, W_r, gn_weight, gn_bias, gn_mean_scale):
        import jax, jax.numpy as jnp
        import numpy as np
        N_NODES = 6250
        N_EDGES = 100000
        HIDDEN = 128
        N_GRAPHS = 32
        EPS = 1e-05
        src, dst = (edge_index[0], edge_index[1])
        n = x.shape[0]
        msg_sum = jax.ops.segment_sum(x[src], dst, num_segments=n)
        deg = jax.ops.segment_sum(jnp.ones((src.shape[0],), x.dtype), dst, num_segments=n)
        agg = msg_sum / jnp.maximum(deg, 1.0)[:, None]
        out = agg @ W_l + b_l + x @ W_r
        g_cnt = jax.ops.segment_sum(jnp.ones((n,), x.dtype), batch, num_segments=N_GRAPHS)[:, None]
        g_cnt = jnp.maximum(g_cnt, 1.0)
        mean = jax.ops.segment_sum(out, batch, num_segments=N_GRAPHS) / g_cnt
        sub = out - gn_mean_scale * mean[batch]
        var = jax.ops.segment_sum(sub * sub, batch, num_segments=N_GRAPHS) / g_cnt
        normed = gn_weight * sub / jnp.sqrt(var[batch] + EPS) + gn_bias
        return jax.nn.gelu(normed, approximate=False) + x

    def _L2_gnn_ref(h, src, dst, W, b):
        import jax, jax.numpy as jnp
        import numpy as np
        N_NODES = 12500
        N_EDGES = 200000
        D_IN = 128
        D_OUT = 128
        n = h.shape[0]
        msg = h[src]
        summed = jax.ops.segment_sum(msg, dst, num_segments=n)
        deg = jax.ops.segment_sum(jnp.ones((src.shape[0],), h.dtype), dst, num_segments=n)
        h_N = summed / jnp.maximum(deg, 1.0)[:, None]
        h_total = jnp.concatenate([h, h_N], axis=1)
        return h_total @ W.T + b

    def _L3_gnn_ref(x, edge_index, edge_attr, W, a):
        import jax, jax.numpy as jnp
        import numpy as np
        N_NODES = 6250
        N_EDGES = 100000
        IN_F = 128
        OUT_F = 32
        HEADS = 4
        EDGE_DIM = 8
        ALPHA = 0.2
        n_nodes = x.shape[0]
        out_f = W.shape[2]
        src, dst = (edge_index[0], edge_index[1])
        xt = jnp.einsum('ni,hio->nho', x, W)
        x_src = xt[src]
        x_dst = xt[dst]
        av = a[..., 0]
        a_s = av[:, :out_f]
        a_d = av[:, out_f:2 * out_f]
        a_e = av[:, 2 * out_f:]
        e = jnp.einsum('eho,ho->eh', x_src, a_s) + jnp.einsum('eho,ho->eh', x_dst, a_d) + edge_attr @ a_e.T
        e = jnp.where(e > 0, e, ALPHA * e)
        max_e = jax.ops.segment_max(e, dst, num_segments=n_nodes)
        max_e = jnp.where(jnp.isneginf(max_e), jnp.zeros_like(max_e), max_e)
        exp_e = jnp.exp(e - max_e[dst])
        sum_exp = jax.ops.segment_sum(exp_e, dst, num_segments=n_nodes)
        attention = exp_e / (sum_exp[dst] + 1e-10)
        weighted = x_src * attention[:, :, None]
        out = jax.ops.segment_sum(weighted, dst, num_segments=n_nodes)
        return out.reshape(n_nodes, -1)
    edge_index = jnp.stack([src, dst])
    batch0 = jnp.zeros((6250,), jnp.int32)
    h = jnp.maximum(_layernorm(x, axis=-1), 0.0)
    x = x + _L0_gnn_ref(h, edge_index, edge_attr_128, L0_gnn_u, batch0, L0_gnn_W1, L0_gnn_b1, L0_gnn_W2, L0_gnn_b2)
    h = jnp.maximum(_layernorm(x, axis=-1), 0.0)
    x = x + _L1_gnn_ref(h, edge_index, batch0, L1_gnn_W_l, L1_gnn_b_l, L1_gnn_W_r, L1_gnn_gn_weight, L1_gnn_gn_bias, L1_gnn_gn_mean_scale)
    h = jnp.maximum(_layernorm(x, axis=-1), 0.0)
    x = x + _L2_gnn_ref(h, src, dst, L2_gnn_W, L2_gnn_b)
    h = jnp.maximum(_layernorm(x, axis=-1), 0.0)
    x = x + _L3_gnn_ref(h, edge_index, edge_attr_8, L3_gnn_W, L3_gnn_a)
    return x

_drawn_inputs = setup_inputs


def setup_inputs(seed=0):
    import zlib

    import numpy as np

    out = dict(_drawn_inputs(seed))
    spreads = {'L0_gnn_b1': (0.0, 0.296),
     'L0_gnn_b2': (0.0, 0.1),
     'L1_gnn_b_l': (0.0, 0.8),
     'L1_gnn_gn_weight': (1.0, 0.2),
     'L1_gnn_gn_bias': (0.0, 0.401),
     'L1_gnn_gn_mean_scale': (1.0, 0.2),
     'L2_gnn_b': (0.0, 0.274)}
    factors = {'edge_attr_8': 7.999, 'L0_gnn_u': 3.598, 'L3_gnn_a': 3.528}
    for name, (base, spread) in spreads.items():
        noise = np.random.default_rng([zlib.crc32(name.encode()), seed]).standard_normal(out[name].shape)
        drawn = base * np.exp(spread * noise) if base else spread * noise
        out[name] = jnp.asarray(drawn.astype(out[name].dtype))
    for name, factor in factors.items():
        out[name] = (out[name] * factor).astype(out[name].dtype)
    return out
```

```python
from contextlib import ExitStack

import numpy as np

import concourse.bass as bass
from concourse import mybir

F32 = mybir.dt.float32
BF16 = mybir.dt.bfloat16
I32 = mybir.dt.int32
ALU = mybir.AluOpType
ACT = mybir.ActivationFunctionType
AX = mybir.AxisListType
DVE_ENGINE = (mybir.EngineType.DVE,)
SP_ENGINE = (mybir.EngineType.SP,)

P = 128
N, F = 6250, 128
E = 200000
HID = 1024
KH = HID // P
HEADS, HO, EA = 4, 32, 8
HW = HO + 1
RW = HEADS * (HW + 1)
NT = -(-N // P)
LAST = N - (NT - 1) * P
G = 2
W = G * P
FULL = E // W
NG = -(-E // W)
DUP = NG * W - E
NS = NG + NT - 1
U = 8
D = 4
IT = -(-NS // U)
NB = -(-IT * U // P)
NSP = NB * P
CT = 4
NC = NT // CT
FAR = 1.0e6
PEN = 3.0e38
BIG = 1.0e38
EPS = 1e-5


class Count:

    def __init__(self, sem):
        self.sem, self.n = sem, 0

    def inc(self, ins, by=1):
        ins.then_inc(self.sem, by)
        self.n += by
        return self.n


def gnn_program(nc, x, src, dst, edge_attr, edge_attr8, u0, W1, b1, W2, b2, Wl, bl, Wr, gw, gb, gms,
                Wsage, bsage, Wgat, agat, out):
    ctx = ExitStack()
    with ctx:
        def sb(name, shape, dt=F32):
            return ctx.enter_context(nc.sbuf_tensor(name, shape, dt))

        used_sems = []

        def sem(name):
            used_sems.append(nc.alloc_semaphore(name=name))
            return used_sems[-1]

        def turn_of(t, j):
            return t * (U // D) + j // D + 1

        def recycle_semaphores():
            nc.clear_and_free_semaphores(used_sems)
            used_sems.clear()
            nc.all_engine_barrier()

        def dram(name, shape, dt=F32):
            return nc.dram_tensor(name, shape, dt, kind="Internal").ap()

        src_rows = dram("src_rows", [NG, W], I32)
        dst_rows = dram("dst_rows", [NG, W], I32)
        prev_rows = dram("prev_rows", [NG, W], I32)
        next_rows = dram("next_rows", [NG, W], I32)
        ea8_rows = dram("ea8_rows", [NG, W * EA])
        pen_rows = dram("pen_rows", [NSP, W], BF16)
        h_rows = dram("h_rows", [NT * P, F])
        xt_rows = dram("xt_rows", [NT * P, RW])

        x_sb = sb("x_sb", [P, NT, F])
        h_sb = sb("h_sb", [P, NT, F])
        ident = sb("ident", [P, P])
        iota_n = sb("iota_n", [P, P])
        node_key = sb("node_key", [P, G, NSP])
        last_flag = sb("last_flag", [P, G, NSP])
        src_idx = sb("src_idx", [P, G, NSP], I32)
        nt_row = sb("nt_row", [1, U + NSP], I32)
        base_row = sb("base_row", [1, NSP], I32)
        deg = sb("deg", [P, NT])
        rdeg = sb("rdeg", [P, NT])
        stats = sb("stats", [P, NT, 6])
        mv = sb("mv", [P, NT, 2])
        veps = sb("veps", [P, NT])
        std = sb("std", [P, NT])
        rstd = sb("rstd", [P, NT])
        nmr = sb("nmr", [P, NT])
        bias_bc = sb("bias_bc", [P, 2, F])
        small = sb("small", [P, 64])
        a_bc = sb("a_bc", [P, HEADS * (2 * HO + EA)])
        eg_col = sb("eg_col", [P, NB], I32)
        acc = sb("acc", [P, NT * (2 * F + 1)])
        idx_now = sb("idx_now", [P, U, G], I32)
        step_mem = sb("step_mem", [P, U * G * RW + 3 * D * G * P + D * W + D * W // 2])
        o1 = U * G * RW
        edge_buf = step_mem[:, 0:o1].rearrange("p (u g f) -> p u g f", u=U, g=G)
        onehot = step_mem[:, o1:o1 + D * G * P].rearrange("p (u g n) -> p u g n", u=D, g=G)
        o2 = o1 + D * G * P
        onehot_last = step_mem[:, o2:o2 + D * G * P].rearrange("p (u g n) -> p u g n", u=D, g=G)
        o3 = o2 + D * G * P
        lastmax = step_mem[:, o3:o3 + D * G * F].rearrange("p (u g f) -> p u g f", u=D, g=G)
        o4 = o3 + D * G * F
        scan_buf = step_mem[:, o4:o4 + D * W].rearrange("p (u w) -> p u w", u=D)
        o5 = o4 + D * W
        pen_buf = step_mem[:, o5:o5 + D * W // 2].bitcast(BF16).rearrange("p (u w) -> p u w", u=D)
        stage = step_mem[:, 0:CT * 4 * F].rearrange("p (i k f) -> p i k f", i=CT, k=4)
        gelu_t = step_mem[:, CT * 4 * F:CT * 5 * F]
        CW = CT * P
        WORK = 4 * HID + KH * F + 4 * CW + KH * CW
        work = sb("work", [P, WORK])
        score_e = work[:, 0:HEADS * G * NSP].rearrange("p (h g s) -> p h g s", h=HEADS, g=G)

        bank = [ctx.enter_context(nc.psum_tensor(f"bank{i}", [P, 512], F32)) for i in range(8)]

        def sv(c):
            return small[:, c:c + 1]

        TW = NB * W
        raw = acc[:, 0:4 * TW].bitcast(I32).rearrange("p (k c w) -> p k c w", k=4, c=NB)
        fl = work[:, 0:5 * TW].rearrange("p (k c w) -> p k c w", k=5, c=NB)
        pen_w = acc[:, 4 * TW:4 * TW + TW // 2].bitcast(BF16).rearrange("p (c w) -> p c w", c=NB)
        keyf, srcf, eqf, lastf = fl[:, 0], fl[:, 1], fl[:, 2], fl[:, 3]
        o = 5 * TW
        tgrid = work[:, o:o + NT - 1]
        scol = work[:, o + 64:o + 64 + NB]
        ldf = work[:, o + 80:o + 80 + NB]
        ntc = work[:, o + 96:o + 96 + NB]
        egf = work[:, o + 112:o + 112 + NB]
        kill1 = work[:, o + 128:o + 128 + NB]
        koff = work[:, o + 144:o + 144 + NB]
        ldi = work[:, o + 160:o + 160 + NB].bitcast(I32)
        onesk = work[:, o + 176:o + 177]
        thr = work[:, o + 177:o + 178]
        consts_i = work[:, o + 178:o + 180].bitcast(I32)
        edf = work[:, o + 192:o + 240]
        srow = x_sb[:, 0:NB, :].rearrange("p a b -> p (a b)")
        ind = x_sb[:, NB:2 * NB, :].rearrange("p a b -> p (a b)")
        ntf = x_sb[0:1, 2 * NB:3 * NB, :].rearrange("p a b -> p (a b)")
        gfr = x_sb[0:1, 3 * NB:4 * NB, :].rearrange("p a b -> p (a b)")
        befr = x_sb[0:1, 4 * NB:5 * NB, :].rearrange("p a b -> p (a b)")
        less = x_sb[:, 5 * NB:5 * NB + NB, :]

        rows_in, small_in, consts = sem("rows_in"), sem("small_in"), sem("consts")
        iotas, ident_zero, ident_made = sem("iotas"), sem("ident_zero"), sem("ident_made")
        before_mm, col_mm, row_mm = sem("before_mm"), sem("col_mm"), sem("row_mm")
        t_dve, eg_ready, raw_in = sem("t_dve"), sem("eg_ready"), sem("raw_in")
        keys_ready, turned, turned_used, pen_out = sem("keys_ready"), sem("turned"), sem("turned_used"), sem("pen_out")
        cut = FULL * W

        def flat(a):
            return a.rearrange("a b -> (a b)")

        with nc.Block() as block:
            @block.sync
            def _(sp):
                with nc.allow_non_contiguous_dma(reason="one last destination of each group"):
                    for c in range(NB):
                        n = min(P, FULL - c * P)
                        if c == 0:
                            sp.wait_ge(consts, 1)
                        sp.dma_start(ldi[0:n, c:c + 1],
                                     dst[c * P * W:(c * P + n) * W].rearrange("(p w) -> p w", w=W)[:, W - 1:W]
                                     ).then_inc(small_in, 16)
                sp.dma_start(flat(src_rows)[0:cut].rearrange("(a b) -> a b", a=11), src[0:cut].rearrange("(a b) -> a b", a=11)).then_inc(rows_in, 16)
                sp.dma_start(src_rows[FULL:NG, :], src[E - W:E].rearrange("(a b) -> a b", a=1)).then_inc(rows_in, 16)
                sp.dma_start(flat(dst_rows)[0:cut].rearrange("(a b) -> a b", a=11), dst[0:cut].rearrange("(a b) -> a b", a=11)).then_inc(rows_in, 16)
                sp.dma_start(dst_rows[FULL:NG, :], dst[E - W:E].rearrange("(a b) -> a b", a=1)).then_inc(rows_in, 16)
                sp.dma_start(flat(prev_rows)[1:cut].rearrange("(a b) -> a b", a=15), dst[0:cut - 1].rearrange("(a b) -> a b", a=15)).then_inc(rows_in, 16)
                sp.dma_start(prev_rows[FULL:NG, :], dst[E - W - 1:E - 1].rearrange("(a b) -> a b", a=1)).then_inc(rows_in, 16)
                sp.dma_start(flat(next_rows)[0:cut].rearrange("(a b) -> a b", a=11), dst[1:cut + 1].rearrange("(a b) -> a b", a=11)).then_inc(rows_in, 16)
                sp.dma_start(next_rows[FULL:NG, 0:W - 1], dst[E - W + 1:E].rearrange("(a b) -> a b", a=1)).then_inc(rows_in, 16)
                sp.wait_ge(consts, 3)
                sp.dma_start(prev_rows[0:1, 0:1], consts_i[0:1, 0:1]).then_inc(rows_in, 16)
                sp.dma_start(next_rows[FULL:NG, W - 1:W], consts_i[0:1, 1:2]).then_inc(rows_in, 16)
                for a in range(11):
                    n = FULL // 11
                    sp.dma_start(ea8_rows[a * n:(a + 1) * n, :],
                                 edge_attr8[a * n * W:(a + 1) * n * W, :].rearrange("(a w) k -> a (w k)", w=W)).then_inc(rows_in, 16)
                sp.dma_start(ea8_rows[FULL:NG, :], edge_attr8[E - W:E, :].rearrange("(a w) k -> a (w k)", w=W)).then_inc(rows_in, 16)
                sp.wait_ge(keys_ready, 1)
                sp.dma_start(pen_rows.rearrange("(c p) w -> p c w", p=P), pen_w).then_inc(pen_out, 16)
                sp.wait_ge(pen_out, 16)

            @block.gpsimd
            def _(pool):
                pool.memset(ldi, 2 ** 30).then_inc(consts, 1)
                pool.memset(consts_i[:, 0:1], -1).then_inc(consts, 1)
                pool.memset(consts_i[:, 1:2], 2 ** 20).then_inc(consts, 1)
                pool.memset(ident[:, :], 0.0).then_inc(ident_zero, 1)
                pool.iota(tgrid, [[P, NT - 1]], base=P, channel_multiplier=0,
                          allow_small_or_imprecise_dtypes=True).then_inc(iotas, 1)
                pool.iota(srow, [[1, NSP]], base=0, channel_multiplier=0,
                          allow_small_or_imprecise_dtypes=True).then_inc(iotas, 1)
                pool.iota(scol, [[P, NB]], base=0, channel_multiplier=1,
                          allow_small_or_imprecise_dtypes=True).then_inc(iotas, 1)
                pool.iota(thr, [[0, 1]], base=1, channel_multiplier=1,
                          allow_small_or_imprecise_dtypes=True).then_inc(iotas, 1)
                pool.iota(iota_n[:, :], [[1, P]], base=0, channel_multiplier=0,
                          allow_small_or_imprecise_dtypes=True).then_inc(iotas, 1)
                pool.memset(onesk, 1.0).then_inc(iotas, 1)
                pool.wait_ge(ident_zero, 1)
                pool.affine_select(out=ident[:, :], in_=ident[:, :], compare_op=ALU.not_equal, fill=1.0,
                                   base=0, pattern=[[-1, P]], channel_multiplier=1).then_inc(ident_made, 1)
                pool.wait_ge(rows_in, 16 * 22)
                pool.wait_ge(eg_ready, 1)
                for c in range(NB):
                    for k, rows in enumerate((dst_rows, prev_rows, next_rows, src_rows)):
                        pool.indirect_dma_start(raw[:, k, c, :], None, rows[:, :],
                                                bass.IndirectOffsetOnAxis(ap=eg_col[:, c:c + 1], axis=0)
                                                ).then_inc(raw_in, 16)

            @block.tensor
            def _(pe):
                for c in range(NB):
                    if c == 0:
                        pe.wait_ge(t_dve, 1 + NB)
                    last = pe.matmul(bank[0][0:NT - 1, 0:1], less[:, c, 0:NT - 1], onesk, start=(c == 0), stop=(c == NB - 1))
                last.then_inc(before_mm, 1)
                pe.wait_ge(t_dve, 3 + NB)
                for c in range(NB):
                    last = pe.matmul(bank[1][:, c:c + 1], ind[0:NT - 1, c * P:(c + 1) * P], onesk[0:NT - 1, :],
                                     start=True, stop=True)
                last.then_inc(col_mm, 1)
                for i in range(2):
                    last = pe.matmul(bank[2 + i][0:1, 0:NSP // 2], onesk[0:NT - 1, :],
                                     ind[0:NT - 1, i * NSP // 2:(i + 1) * NSP // 2], start=True, stop=True)
                last.then_inc(row_mm, 1)
                pe.wait_ge(ident_made, 1)
                pe.wait_ge(keys_ready, 1)
                for c in range(NB):
                    if c >= 2:
                        pe.wait_ge(turned_used, 3 * (c - 1))
                    for k, table in enumerate((keyf, lastf, srcf)):
                        b = bank[k + 3 * (c % 2)] if c % 2 == 0 else bank[3 + k]
                        for g in range(G):
                            last = pe.transpose(b[:, g * P:(g + 1) * P], table[:, c, g * P:(g + 1) * P], ident[:, :])
                        last.then_inc(turned, 1)

            @block.vector
            def _(dve):
                step = Count(t_dve)

                def link(ins):
                    dve.wait_ge(t_dve, step.inc(ins))

                dve.wait_ge(iotas, 6)
                dve.wait_ge(small_in, 16 * NB)
                link(dve.tensor_copy(ldf, ldi))
                for c in range(NB):
                    step.inc(dve.tensor_scalar(less[:, c, 0:NT - 1], tgrid, ldf[:, c:c + 1], None, ALU.is_gt))
                dve.wait_ge(before_mm, 1)
                link(dve.tensor_tensor(thr[0:NT - 1, :], bank[0][0:NT - 1, 0:1], thr[0:NT - 1, :], ALU.add))
                step.inc(dve.tensor_scalar(ind[0:NT - 1, :], srow[0:NT - 1, :], thr[0:NT - 1, :], None, ALU.is_ge))
                dve.wait_ge(col_mm, 1)
                link(dve.tensor_copy(ntc, bank[1][:, 0:NB]))
                link(dve.tensor_tensor(egf, scol, ntc, ALU.subtract))
                link(dve.tensor_scalar(kill1, egf, float(NG - 1), FAR, ALU.is_equal, ALU.mult))
                link(dve.tensor_scalar(koff, egf, float(NG - 1), FAR, ALU.is_gt, ALU.mult))
                link(dve.scalar_tensor_tensor(out=koff, in0=ntc, scalar=-float(P), in1=koff, op0=ALU.mult, op1=ALU.add))
                dve.tensor_scalar(eg_col[:, :], egf, float(NG - 1), None, ALU.min).then_inc(eg_ready, 1)
                dve.wait_ge(row_mm, 1)
                for i in range(2):
                    link(dve.tensor_copy(ntf[:, i * NSP // 2:(i + 1) * NSP // 2], bank[2 + i][0:1, 0:NSP // 2]))
                step.inc(dve.memset(nt_row[:, 0:U], 0))
                link(dve.tensor_copy(nt_row[:, U:U + NSP], ntf))
                link(dve.tensor_tensor(gfr, srow[0:1, :], ntf, ALU.subtract))
                link(dve.tensor_scalar(befr, gfr, float(W), float(E - W), ALU.mult, ALU.min))
                link(dve.tensor_copy(base_row[:, :], befr))
                dve.wait_ge(raw_in, 16 * 4 * NB)
                for c in range(NB):
                    step.inc(dve.tensor_scalar(keyf[:, c, 0:DUP], raw[:, 0, c, 0:DUP], koff[:, c:c + 1],
                                               kill1[:, c:c + 1], ALU.add, ALU.add))
                    link(dve.tensor_scalar(keyf[:, c, DUP:W], raw[:, 0, c, DUP:W], koff[:, c:c + 1], None, ALU.add))
                link(dve.tensor_copy(srcf, raw[:, 3]))
                link(dve.tensor_tensor(eqf, raw[:, 0], raw[:, 1], ALU.is_equal))
                link(dve.tensor_scalar(pen_w, eqf, PEN, -PEN, ALU.mult, ALU.add))
                link(dve.tensor_tensor(eqf, raw[:, 0], raw[:, 2], ALU.is_equal))
                dve.tensor_scalar(lastf, eqf, -1.0, 1.0, ALU.mult, ALU.add).then_inc(keys_ready, 1)
                for c in range(NB):
                    for k, table in enumerate((node_key, last_flag, src_idx)):
                        b = bank[k + 3 * (c % 2)] if c % 2 == 0 else bank[3 + k]
                        dve.wait_ge(turned, 3 * c + k + 1)
                        dve.tensor_copy(table[:, :, c * P:(c + 1) * P],
                                        b[:, 0:W].rearrange("p (g s) -> p g s", g=G)).then_inc(turned_used, 1)

        def layer_norm(tag, load_x=False, loads=(), store=False):
            x_in, zeroed = sem(f"x_in{tag}"), sem(f"x_zeroed{tag}")
            ln_dve, ln_std, ln_norm, ln_h = (sem(f"{s}{tag}") for s in ("ln_dve", "ln_std", "ln_norm", "ln_h"))
            h_out, weights_in = sem(f"h_out{tag}"), sem(f"weights_in{tag}")
            with nc.Block() as block:
                @block.sync
                def _(sp):
                    if load_x:
                        sp.dma_start(x_sb[:, 0:NT - 1, :], x[0:(NT - 1) * P, :].rearrange("(t p) f -> p t f", p=P)).then_inc(x_in, 16)
                        sp.wait_ge(zeroed, 1)
                        sp.dma_start(x_sb[0:LAST, NT - 1, :], x[(NT - 1) * P:N, :]).then_inc(x_in, 16)
                    for to, frm in loads:
                        sp.dma_start(to, frm).then_inc(weights_in, 16)
                    if store:
                        sp.wait_ge(ln_h, NT)
                        sp.dma_start(h_rows.rearrange("(t p) f -> p t f", p=P), h_sb[:, :, :]).then_inc(h_out, 16)
                        sp.wait_ge(h_out, 16)
                    if loads:
                        sp.wait_ge(weights_in, 16 * len(loads))

                @block.vector
                def _(dve):
                    step = Count(ln_dve)

                    def link(ins):
                        dve.wait_ge(ln_dve, step.inc(ins))

                    if load_x:
                        dve.memset(x_sb[:, NT - 1, :], 0.0).then_inc(zeroed, 1)
                        dve.wait_ge(x_in, 32)
                    for t in range(NT):
                        step.inc(dve.bn_stats(stats[:, t, :], x_sb[:, t, :]))
                    for t in range(NT):
                        dve.wait_ge(ln_dve, t + 1)
                        step.inc(dve.bn_aggr(mv[:, t, :], stats[:, t, :]))
                    dve.wait_ge(ln_dve, step.n)
                    dve.tensor_scalar(veps[:, :], mv[:, :, 1], EPS, None, ALU.add).then_inc(ln_std, 1)
                    dve.wait_ge(ln_std, 2)
                    link(dve.reciprocal(rstd[:, :], std[:, :]))
                    dve.scalar_tensor_tensor(out=nmr[:, :], in0=mv[:, :, 0], scalar=-1.0, in1=rstd[:, :],
                                             op0=ALU.mult, op1=ALU.mult).then_inc(ln_norm, 1)

                @block.scalar
                def _(act):
                    act.wait_ge(ln_std, 1)
                    act.activation(std[:, :], veps[:, :], ACT.Sqrt).then_inc(ln_std, 1)
                    act.wait_ge(ln_norm, 1)
                    for t in range(NT):
                        act.activation(h_sb[:, t, :], x_sb[:, t, :], ACT.Relu, bias=nmr[:, t:t + 1],
                                       scale=rstd[:, t:t + 1]).then_inc(ln_h, 1)

        w1_sb = work[:, 0:4 * HID].rearrange("p (k n) -> p k n", k=4)
        w2_sb = work[:, 4 * HID:4 * HID + KH * F].rearrange("p (j n) -> p j n", j=KH)
        b1_sb = small[:, 0:KH]
        w1u_sb = small[:, KH:2 * KH]
        u_bc = sv(2 * KH)
        bias1 = small[:, 3 * KH:4 * KH]
        with nc.allow_non_contiguous_dma(reason="bias columns, once"):
            layer_norm("0", load_x=True, loads=[
                (w1_sb, W1[0:4 * P, :].rearrange("(k p) n -> p k n", p=P)),
                (w2_sb, W2.rearrange("(j p) n -> p j n", p=P)),
                (b1_sb, b1.rearrange("(j p) -> p j", p=P)),
                (w1u_sb, W1[4 * P, :].rearrange("(j p) -> p j", p=P)),
                (u_bc, u0[0:1, 0:1].broadcast_to([P, 1])),
                (bias_bc[:, 0, :], b2.rearrange("(a f) -> a f", a=1).broadcast_to([P, F])),
                (bias_bc[:, 1, :], bsage.rearrange("(a f) -> a f", a=1).broadcast_to([P, F])),
            ])

        def run_steps(eng, stages, before=None):
            def at(t, j, end, loaded):
                for fn, d in stages:
                    tt, jj = t + (j - d) // U, (j - d) % U
                    if isinstance(tt, int) and not 0 <= tt < end:
                        continue
                    fn(tt, jj, loaded[d][j] if loaded is not None and d in loaded else None)

            def iteration(t, end=IT, slots=U):
                loaded = before(t) if before else None
                for j in range(slots):
                    at(t, j, end, loaded)

            iteration(0)
            with eng.Fori(1, IT) as t:
                iteration(t)
            behind = max(d for _, d in stages)
            if behind:
                iteration(IT, IT, behind)

        def tiles_of_steps(t, behind):
            got = {}
            for d in behind:
                _, got[d] = nc.values_load_multi_w_load_instructions(
                    nt_row[0:1, bass.ds(t * U + (U - d), U)], engines=DVE_ENGINE, min_val=0, max_val=NT - 1,
                    skip_runtime_bounds_check_because="the table counts tiles")
            return got

        A0 = 2 * F + 1
        acc0 = acc[:, :].rearrange("p (t f) -> p t f", t=NT)
        edges_in = [sem(f"edges_in{j}") for j in range(U)]
        pen_in = [sem(f"pen_in{j}") for j in range(D)]
        cleared, one_hot, one_hot_last = sem("cleared"), sem("one_hot"), sem("one_hot_last")
        edges_turned, scanned, max_turned, max_copied = sem("edges_turned"), sem("scanned"), sem("max_turned"), sem("max_copied")
        edges_used, sums_ready, sums_added, bias_made = sem("edges_used"), sem("sums_ready"), sem("sums_added"), sem("bias_made")
        xT = [bank[0][:, 0:W], bank[1][:, 0:W]]
        sT = [bank[2][:, 0:W], bank[3][:, 0:W]]
        sums = [bank[4 + j % D] for j in range(U)]

        with nc.Block() as block:
            @block.sync
            def _(sp):
                def load(t, j, _):
                    s = t * U + j
                    sp.wait_ge(edges_used, s + 1)
                    sp.dma_start(edge_buf[:, j, :, 0:F],
                                 edge_attr[bass.ds(bases[j], W), :].rearrange("(g p) f -> p g f", p=P)).then_inc(edges_in[j], 16)
                    sp.wait_ge(scanned, s + 1)
                    sp.dma_start(pen_buf[:, j % D, :], pen_rows[bass.ds(s, 1), :].broadcast_to([P, W])).then_inc(pen_in[j % D], 16)

                with sp.Fori(0, IT) as t:
                    _, bases = nc.values_load_multi_w_load_instructions(
                        base_row[0:1, bass.ds(t * U, U)], engines=SP_ENGINE, min_val=0, max_val=E - W,
                        skip_runtime_bounds_check_because="the table is cut at E - W")
                    for j in range(U):
                        load(t, j, None)

            @block.gpsimd
            def _(pool):
                pool.memset(edge_buf[:, :, :, F:F + 1], 1.0).then_inc(cleared, 1)
                pool.memset(acc[:, :], 0.0).then_inc(cleared, 1)

            @block.tensor
            def _(pe):
                pe.sem_inc(edges_used, U)
                pe.sem_inc(sums_ready, D)
                pe.wait_ge(cleared, 2)

                def turn_and_sum(t, j, _):
                    s = t * U + j
                    pe.wait_ge(edges_in[j], 16 * (t + 1))
                    pe.wait_ge(scanned, s + D - 1)
                    for g in range(G):
                        last = pe.transpose(xT[j % 2][:, g * P:(g + 1) * P], edge_buf[:, j, g, 0:F], ident[:, :])
                    last.then_inc(edges_turned, 1)
                    pe.wait_ge(one_hot, s + 1)
                    pe.wait_ge(sums_added, s + 1)
                    for g in range(G):
                        last = pe.matmul(sums[j][:, 0:F + 1], onehot[:, j % D, g, :], edge_buf[:, j, g, 0:F + 1],
                                         start=(g == 0), stop=(g == G - 1))
                    last.then_inc(edges_used, 1)

                def maxima(t, j, _):
                    s = t * U + j
                    pe.wait_ge(scanned, s + D + 1)
                    pe.wait_ge(max_copied, s + 1)
                    for g in range(G):
                        last = pe.transpose(sT[j % 2][:, g * P:(g + 1) * P], scan_buf[:, j % D, g * P:(g + 1) * P], ident[:, :])
                    last.then_inc(max_turned, 1)
                    pe.wait_ge(max_copied, s + 3)
                    pe.wait_ge(one_hot_last, s + 1)
                    for g in range(G):
                        last = pe.matmul(sums[j][:, F + 1:A0], onehot_last[:, j % D, g, :], lastmax[:, j % D, g, :],
                                         start=(g == 0), stop=(g == G - 1))
                    last.then_inc(sums_ready, 1)

                run_steps(pe, [(turn_and_sum, 0), (maxima, 1)])

            @block.scalar
            def _(act):
                act.sem_inc(max_copied, 2)
                act.activation(bias1, w1u_sb, ACT.Copy, scale=u_bc).then_inc(bias_made, 1)
                with act.Fori(0, IT) as t:
                    for j in range(U):
                        s = t * U + j
                        act.wait_ge(one_hot, s + 1)
                        act.wait_ge(sums_ready, s + 1)
                        for g in range(G):
                            last = act.activation(onehot_last[:, j % D, g, :], onehot[:, j % D, g, :], ACT.Copy,
                                                  scale=last_flag[:, g, bass.ds(s, 1)])
                        last.then_inc(one_hot_last, 1)
                        act.wait_ge(max_turned, s + 1)
                        act.activation(lastmax[:, j % D, :, :], sT[j % 2].rearrange("p (g f) -> p g f", g=G), ACT.Copy).then_inc(max_copied, 1)

            @block.vector
            def _(dve):
                dve.sem_inc(scanned, D)
                dve.sem_inc(sums_added, D)
                dve.wait_ge(bias_made, 1)
                dve.tensor_tensor(bias1, bias1, b1_sb, ALU.add).then_inc(bias_made, 1)
                dve.memset(scan_buf[:, D - 1, W - 1:W], 0.0).then_inc(bias_made, 1)
                dve.wait_ge(bias_made, 3)
                dve.wait_ge(cleared, 2)

                def scan(t, j, _):
                    s = t * U + j
                    dve.wait_ge(edges_used, s + 1 + U - D)
                    if not (isinstance(s, int) and s < D):
                        dve.wait_ge(one_hot_last, s + 1 - D)
                    for g in range(G):
                        last = dve.tensor_scalar(onehot[:, j % D, g, :], iota_n[:, :], node_key[:, g, bass.ds(s, 1)], None, ALU.is_equal)
                    last.then_inc(one_hot, 1)
                    dve.wait_ge(edges_turned, s + 1)
                    dve.wait_ge(pen_in[j % D], 16 * turn_of(t, j))
                    dve.wait_ge(scanned, s + D)
                    if not (isinstance(s, int) and s < D):
                        dve.wait_ge(max_turned, s + 1 - D)
                    dve.tensor_tensor_scan(scan_buf[:, j % D, :], pen_buf[:, j % D, :], xT[j % 2],
                                           scan_buf[:, (j - 1) % D, W - 1:W], ALU.add, ALU.max).then_inc(scanned, 1)

                def add(t, j, tile):
                    s = t * U + j
                    dve.wait_ge(sums_ready, s + D + 1)
                    dve.wait_ge(sums_added, s + D)
                    row = acc0[:, bass.ds(tile, 1), :].rearrange("p a f -> p (a f)")
                    dve.tensor_tensor(row, row, sums[j][:, 0:A0], ALU.add).then_inc(sums_added, 1)

                run_steps(dve, [(scan, 0), (add, 2)], before=lambda t: tiles_of_steps(t, [2]))

        turned_sb = work[:, 4 * HID + KH * F:4 * HID + KH * F + 4 * CW].rearrange("p (k n) -> p k n", k=4)
        gelu_sb = work[:, 4 * HID + KH * F + 4 * CW:WORK].rearrange("p (j n) -> p j n", j=KH)

        def chunks(eng, body):
            with eng.Fori(0, NC) as c:
                body(c, CT)
            for c in range(NC, NC + NT - NC * CT):
                body(NC, NT - NC * CT)

        def tiles(c, n):
            return bass.ds(c * CT, n)

        class Dense:

            def __init__(self, tag, K):
                self.K = K
                self.staged, self.copied_in, self.turned, self.copied, self.out, self.added = (
                    sem(f"{tag}_{s}") for s in ("staged", "copied_in", "turned", "copied", "out", "added"))

        d0 = Dense("mlp", 4)
        hid_ready, hid_done, acc_rd = sem("hid_ready"), sem("hid_done"), sem("rdeg_made")
        b2_bc = bias_bc[:, 0, :].rearrange("p (a f) -> p a f", a=1)
        bs_bc = bias_bc[:, 1, :].rearrange("p (a f) -> p a f", a=1)
        with nc.Block() as block:
            @block.gpsimd
            def _(pool):
                def copy_in(c, n):
                    pool.wait_ge(d0.turned, 4 * c + 4)
                    pool.tensor_copy(stage[:, 0:n, 0, :], h_sb[:, tiles(c, n), :]).then_inc(d0.copied_in, 1)
                    pool.tensor_copy(stage[:, 0:n, 1, :], acc0[:, tiles(c, n), 0:F]).then_inc(d0.copied_in, 1)
                    pool.tensor_copy(stage[:, 0:n, 2, :], acc0[:, tiles(c, n), F + 1:A0]).then_inc(d0.copied_in, 1)

                chunks(pool, copy_in)

            @block.tensor
            def _(pe):
                pe.sem_inc(d0.turned, 4)
                pe.sem_inc(d0.out, 1)

                def chunk(c, n):
                    pe.wait_ge(d0.staged, c + 1)
                    pe.wait_ge(d0.copied_in, 3 * c + 3)
                    for k in range(4):
                        for i in range(n):
                            last = pe.transpose(bank[k][:, i * P:(i + 1) * P], stage[:, i, k, :], ident[:, :])
                        last.then_inc(d0.turned, 1)
                    pe.wait_ge(d0.copied, 4 * c + 4)
                    for j in range(KH):
                        pe.wait_ge(hid_done, KH * c + j + 1)
                        for k in range(4):
                            last = pe.matmul(bank[4 + j % 2][:, 0:n * P], w1_sb[:, k, j * P:(j + 1) * P],
                                             turned_sb[:, k, 0:n * P], start=(k == 0), stop=(k == 3))
                        last.then_inc(hid_ready, 1)
                    pe.wait_ge(hid_done, KH * c + KH + 2)
                    pe.wait_ge(d0.added, c + 1)
                    for i in range(n):
                        for j in range(KH):
                            last = pe.matmul(bank[6][:, i * F:(i + 1) * F], gelu_sb[:, j, i * P:(i + 1) * P],
                                             w2_sb[:, j, :], start=(j == 0), stop=(j == KH - 1))
                    last.then_inc(d0.out, 1)

                chunks(pe, chunk)

            @block.scalar
            def _(act):
                act.sem_inc(hid_done, 2)

                def chunk(c, n):
                    for k in range(4):
                        act.wait_ge(d0.turned, 4 * c + 4 + k + 1)
                        act.activation(turned_sb[:, k, 0:n * P], bank[k][:, 0:n * P], ACT.Copy).then_inc(d0.copied, 1)
                    act.wait_ge(d0.out, c + 1)
                    for j in range(KH):
                        act.wait_ge(hid_ready, KH * c + j + 1)
                        act.activation(gelu_sb[:, j, 0:n * P], bank[4 + j % 2][:, 0:n * P], ACT.Gelu,
                                       bias=bias1[:, j:j + 1]).then_inc(hid_done, 1)

                chunks(act, chunk)

            @block.vector
            def _(dve):
                dve.sem_inc(d0.added, 1)
                dve.tensor_scalar(deg[:, :], acc0[:, :, F], 1.0, None, ALU.max).then_inc(acc_rd, 1)
                dve.wait_ge(acc_rd, 1)
                dve.reciprocal(rdeg[:, :], deg[:, :]).then_inc(acc_rd, 1)
                dve.wait_ge(acc_rd, 2)

                def mean(c, n):
                    dve.wait_ge(d0.turned, 4 * c + 4)
                    dve.tensor_tensor(stage[:, 0:n, 3, :], acc0[:, tiles(c, n), 0:F],
                                      rdeg[:, tiles(c, n)].rearrange("p (t a) -> p t a", a=1).broadcast_to([P, n, F]),
                                      ALU.mult).then_inc(d0.staged, 1)

                def residual(c, n):
                    xs = x_sb[:, tiles(c, n), :]
                    dve.tensor_tensor(xs, xs, h_sb[:, tiles(c, n), :], ALU.add).then_inc(acc_rd, 1)
                    dve.wait_ge(acc_rd, 2 * c + 3)
                    dve.tensor_tensor(xs, xs, b2_bc.broadcast_to([P, n, F]), ALU.add).then_inc(acc_rd, 1)
                    dve.wait_ge(acc_rd, 2 * c + 4)
                    dve.wait_ge(d0.out, c + 2)
                    dve.tensor_tensor(xs, xs, bank[6][:, 0:n * F].rearrange("p (t f) -> p t f", f=F), ALU.add).then_inc(d0.added, 1)

                def both(c, n):
                    mean(c, n)
                    residual(c, n)

                chunks(dve, both)

        recycle_semaphores()
        layer_norm("1", store=True, loads=[(a_bc[:, :], agat.rearrange("h a b -> (b h a)").rearrange("(b n) -> b n", b=1).broadcast_to([P, HEADS * (2 * HO + EA)]))])

        av = a_bc[:, :].rearrange("p (h a) -> p h a", h=HEADS)
        raw8 = acc[:, 0:2 * W * EA].rearrange("p (b e k) -> p b e k", b=2, k=EA)
        srow8 = acc[:, 2 * W * EA:2 * W * EA + 2 * HEADS * W].rearrange("p (b h e) -> p b h e", b=2, h=HEADS)
        ea_in = [sem("ea_in0"), sem("ea_in1")]
        mac, scores_turned, scores_copied = sem("score_products"), sem("scores_turned"), sem("scores_copied")
        MC = HEADS * EA
        with nc.Block() as block:
            @block.gpsimd
            def _(pool):
                for c in range(NB):
                    if c >= 2:
                        pool.wait_ge(mac, MC * (c - 1))
                    pool.indirect_dma_start(raw8[:, c % 2].rearrange("p e k -> p (e k)"), None, ea8_rows[:, :],
                                            bass.IndirectOffsetOnAxis(ap=eg_col[:, c:c + 1], axis=0)).then_inc(ea_in[c % 2], 16)

            @block.vector
            def _(dve):
                n = 0
                for c in range(NB):
                    dve.wait_ge(ea_in[c % 2], 16 * (c // 2 + 1))
                    if c >= 2:
                        dve.wait_ge(scores_turned, HEADS * (c - 1))
                    for k in range(EA):
                        for h in range(HEADS):
                            a = av[:, h, 2 * HO + k:2 * HO + k + 1]
                            o = srow8[:, c % 2, h, :]
                            if k:
                                dve.wait_ge(mac, n + 1 - HEADS)
                                ins = dve.scalar_tensor_tensor(out=o, in0=raw8[:, c % 2, :, k], scalar=a, in1=o,
                                                               op0=ALU.mult, op1=ALU.add)
                            else:
                                ins = dve.tensor_scalar(o, raw8[:, c % 2, :, k], a, None, ALU.mult)
                            ins.then_inc(mac, 1)
                            n += 1

            @block.tensor
            def _(pe):
                for c in range(NB):
                    pe.wait_ge(mac, MC * (c + 1))
                    for h in range(HEADS):
                        q = c * HEADS + h
                        if q >= 8:
                            pe.wait_ge(scores_copied, q - 7)
                        for g in range(G):
                            last = pe.transpose(bank[q % 8][:, g * P:(g + 1) * P], srow8[:, c % 2, h, g * P:(g + 1) * P], ident[:, :])
                        last.then_inc(scores_turned, 1)

            @block.scalar
            def _(act):
                for c in range(NB):
                    for h in range(HEADS):
                        q = c * HEADS + h
                        act.wait_ge(scores_turned, q + 1)
                        act.activation(score_e[:, h, :, c * P:(c + 1) * P],
                                       bank[q % 8][:, 0:W].rearrange("p (g s) -> p g s", g=G), ACT.Copy).then_inc(scores_copied, 1)

        acc1 = acc[:, 0:NT * F].rearrange("p (t f) -> p t f", t=NT)

        def gather(pool, rows, width, got, index_ready, go):
            with pool.Fori(0, IT) as t:
                for j in range(U):
                    pool.wait_ge(index_ready, t * U + j + 1)
                    pool.sem_inc(go, 1)
                    for g in range(G):
                        pool.indirect_dma_start(edge_buf[:, j, g, 0:width], None, rows[:, :],
                                                bass.IndirectOffsetOnAxis(ap=idx_now[:, j, g:g + 1], axis=0)).then_inc(got[j], 16)

        def place_indices(act, t, j, slots_free, index_ready, go):
            s = t * U + j
            act.wait_ge(slots_free, s + 1)
            act.sem_inc(go, 1)
            act.activation(idx_now[:, j, :], src_idx[:, :, bass.ds(s, 1)].rearrange("p g a -> p (g a)"), ACT.Copy).then_inc(index_ready, 1)

        def sum_sources(tag):
            got = [sem(f"{tag}_rows_in{j}") for j in range(U)]
            placed, go, act_go, hot, used, added, clear = (sem(f"{tag}_{s}") for s in (
                "indices_placed", "go", "act_go", "one_hot", "rows_used", "added", "cleared"))
            with nc.Block() as block:
                @block.gpsimd
                def _(pool):
                    gather(pool, h_rows, F, got, placed, go)

                @block.scalar
                def _(act):
                    with act.Fori(0, IT) as t:
                        for j in range(U):
                            place_indices(act, t, j, used, placed, act_go)

                @block.tensor
                def _(pe):
                    pe.sem_inc(used, U)

                    def total(t, j, _):
                        s = t * U + j
                        pe.wait_ge(got[j], 16 * G * (t + 1))
                        pe.wait_ge(hot, s + 1)
                        pe.wait_ge(added, s + 1)
                        for g in range(G):
                            last = pe.matmul(bank[j % D][:, 0:F], onehot[:, j % D, g, :], edge_buf[:, j, g, 0:F],
                                             start=(g == 0), stop=(g == G - 1))
                        last.then_inc(used, 1)

                    run_steps(pe, [(total, 0)])

                @block.vector
                def _(dve):
                    dve.sem_inc(added, D)
                    dve.memset(acc[:, 0:NT * F], 0.0).then_inc(clear, 1)
                    dve.wait_ge(clear, 1)

                    def hots(t, j, _):
                        s = t * U + j
                        dve.wait_ge(used, s + 1 + U - D)
                        for g in range(G):
                            last = dve.tensor_scalar(onehot[:, j % D, g, :], iota_n[:, :], node_key[:, g, bass.ds(s, 1)], None, ALU.is_equal)
                        last.then_inc(hot, 1)

                    def add(t, j, tile):
                        s = t * U + j
                        dve.wait_ge(used, s + U + 1)
                        dve.wait_ge(added, s + D)
                        row = acc1[:, bass.ds(tile, 1), :].rearrange("p a f -> p (a f)")
                        dve.tensor_tensor(row, row, bank[j % D][:, 0:F], ALU.add).then_inc(added, 1)

                    run_steps(dve, [(hots, 0), (add, 2)], before=lambda t: tiles_of_steps(t, [2]))

        OFF3 = HEADS * G * NSP
        turn2 = work[:, OFF3:OFF3 + 2 * CW].rearrange("p (k n) -> p k n", k=2)
        wt = work[:, OFF3 + 2 * CW:OFF3 + 2 * CW + 4 * F].rearrange("p (k n) -> p k n", k=4)

        def stage_means(dve, d, c, n):
            dve.wait_ge(d.turned, 2 * c + 2)
            dve.tensor_tensor(stage[:, 0:n, 0, :], acc1[:, tiles(c, n), :],
                              rdeg[:, tiles(c, n)].rearrange("p (t a) -> p t a", a=1).broadcast_to([P, n, F]),
                              ALU.mult).then_inc(d.staged, 1)

        def stage_own(pool, d, c, n):
            pool.wait_ge(d.turned, 2 * c + 2)
            pool.tensor_copy(stage[:, 0:n, 1, :], h_sb[:, tiles(c, n), :]).then_inc(d.copied_in, 1)

        def turn_two(pe, d, c, n):
            pe.wait_ge(d.staged, c + 1)
            pe.wait_ge(d.copied_in, c + 1)
            pe.wait_ge(d.copied, 2 * c + 2)
            for k in range(2):
                for i in range(n):
                    last = pe.transpose(bank[k][:, i * P:(i + 1) * P], stage[:, i, k, :], ident[:, :])
                last.then_inc(d.turned, 1)
            pe.wait_ge(d.copied, 2 * c + 4)
            pe.wait_ge(d.added, c + 1)

        def copy_two(act, d, c, n):
            act.wait_ge(d.out, c + 1)
            for k in range(2):
                act.wait_ge(d.turned, 2 * c + 2 + k + 1)
                act.activation(turn2[:, k, 0:n * P], bank[k][:, 0:n * P], ACT.Copy).then_inc(d.copied, 1)

        sum_sources("l1")

        out_t = acc[:, NT * F:NT * F + NT * P]
        d1 = Dense("l1d", 2)
        w_in, n_sum, n_chain, n_sq, n_std, n_ready = (sem(f"l1_{s}") for s in ("weights_in", "sum", "chain", "squares", "std", "norm_ready"))
        g_done, g_turned, g_added = sem("l1_gelu"), sem("l1_gelu_turned"), sem("l1_gelu_added")
        bl_c, gw_c, gb_c, gms_c, tot, mean_c, shift, ssq, var_c, std_c, scale_c, beta_c = (sv(32 + i) for i in range(12))
        with nc.Block() as block:
            @block.sync
            def _(sp):
                sp.dma_start(wt[:, 0, :], Wl).then_inc(w_in, 16)
                sp.dma_start(wt[:, 1, :], Wr).then_inc(w_in, 16)
                with nc.allow_non_contiguous_dma(reason="bias columns, once"):
                    for to, frm in ((bl_c, bl), (gw_c, gw), (gb_c, gb), (gms_c, gms)):
                        sp.dma_start(to, frm.rearrange("(p a) -> p a", a=1)).then_inc(w_in, 16)

            @block.gpsimd
            def _(pool):
                chunks(pool, lambda c, n: stage_own(pool, d1, c, n))

            @block.tensor
            def _(pe):
                pe.sem_inc(d1.turned, 2)
                pe.sem_inc(d1.out, 1)
                pe.wait_ge(w_in, 96)

                def chunk(c, n):
                    turn_two(pe, d1, c, n)
                    for k in range(2):
                        last = pe.matmul(bank[2][:, 0:n * P], wt[:, k, :], turn2[:, k, 0:n * P], start=(k == 0), stop=(k == 1))
                    last.then_inc(d1.out, 1)

                chunks(pe, chunk)
                pe.sem_inc(g_turned, 1)

                def back(c, n):
                    pe.wait_ge(g_done, c + 1)
                    pe.wait_ge(g_added, c + 1)
                    for i in range(n):
                        last = pe.transpose(bank[3][:, i * F:(i + 1) * F], gelu_t[:, i * P:(i + 1) * P], ident[:, :])
                    last.then_inc(g_turned, 1)

                chunks(pe, back)

            @block.scalar
            def _(act):
                act.sem_inc(d1.copied, 2)
                act.sem_inc(d1.added, 1)
                act.wait_ge(w_in, 96)

                def chunk(c, n):
                    copy_two(act, d1, c, n)
                    act.wait_ge(d1.out, c + 2)
                    act.activation(out_t[:, bass.ds(c * CW, n * P)], bank[2][:, 0:n * P], ACT.Identity,
                                   bias=bl_c).then_inc(d1.added, 1)

                chunks(act, chunk)
                act.wait_ge(n_sum, 1)
                act.activation(acc[:, 0:N], out_t[:, 0:N], ACT.Square, bias=shift, accum_out=ssq).then_inc(n_sq, 1)
                act.wait_ge(n_std, 1)
                act.activation(std_c, var_c, ACT.Sqrt).then_inc(n_std, 1)
                act.wait_ge(n_ready, 1)

                def gelu(c, n):
                    act.wait_ge(g_turned, c + 1)
                    act.activation(gelu_t[:, 0:n * P], out_t[:, bass.ds(c * CW, n * P)], ACT.Gelu,
                                   bias=beta_c, scale=scale_c).then_inc(g_done, 1)

                chunks(act, gelu)

            @block.vector
            def _(dve):
                step = Count(n_chain)

                def link(ins):
                    dve.wait_ge(n_chain, step.inc(ins))

                chunks(dve, lambda c, n: stage_means(dve, d1, c, n))
                dve.wait_ge(d1.added, NC + 1 + NT - NC * CT)
                link(dve.tensor_reduce(tot, out_t[:, 0:N], AX.X, ALU.add))
                link(dve.tensor_scalar(mean_c, tot, 1.0 / N, None, ALU.mult))
                dve.scalar_tensor_tensor(out=shift, in0=mean_c, scalar=-1.0, in1=gms_c, op0=ALU.mult, op1=ALU.mult).then_inc(n_sum, 1)
                dve.wait_ge(n_sq, 1)
                dve.tensor_scalar(var_c, ssq, 1.0 / N, EPS, ALU.mult, ALU.add).then_inc(n_std, 1)
                dve.wait_ge(n_std, 2)
                link(dve.reciprocal(std_c, std_c))
                link(dve.tensor_tensor(scale_c, gw_c, std_c, ALU.mult))
                link(dve.tensor_tensor(beta_c, scale_c, shift, ALU.mult))
                dve.tensor_tensor(beta_c, beta_c, gb_c, ALU.add).then_inc(n_ready, 1)
                base = step.n

                def residual(c, n):
                    xs = x_sb[:, tiles(c, n), :]
                    dve.tensor_tensor(xs, xs, h_sb[:, tiles(c, n), :], ALU.add).then_inc(n_chain, 1)
                    dve.wait_ge(n_chain, base + 1 + c)
                    dve.wait_ge(g_turned, c + 2)
                    dve.tensor_tensor(xs, xs, bank[3][:, 0:n * F].rearrange("p (t f) -> p t f", f=F), ALU.add).then_inc(g_added, 1)

                dve.sem_inc(g_added, 1)
                chunks(dve, residual)

        layer_norm("2", store=True)
        sum_sources("l2")

        d2 = Dense("l2d", 2)
        w2_in, w2_turned, w2_copied, x_chain = sem("l2_weights_in"), sem("l2_weights_turned"), sem("l2_weights_copied"), sem("l2_chain")
        w_raw = gelu_t[:, 0:2 * F]
        with nc.Block() as block:
            @block.sync
            def _(sp):
                sp.dma_start(w_raw, Wsage).then_inc(w2_in, 16)

            @block.gpsimd
            def _(pool):
                chunks(pool, lambda c, n: stage_own(pool, d2, c, n))

            @block.tensor
            def _(pe):
                pe.sem_inc(d2.turned, 2)
                pe.sem_inc(d2.out, 1)
                pe.wait_ge(w2_in, 16)
                for k in range(2):
                    last = pe.transpose(bank[3][:, k * F:(k + 1) * F], w_raw[:, k * F:(k + 1) * F], ident[:, :])
                last.then_inc(w2_turned, 1)
                pe.wait_ge(w2_copied, 1)

                def chunk(c, n):
                    turn_two(pe, d2, c, n)
                    for i in range(n):
                        for k in range(2):
                            last = pe.matmul(bank[2][:, i * F:(i + 1) * F], turn2[:, k, i * P:(i + 1) * P], wt[:, 1 - k, :],
                                             start=(k == 0), stop=(k == 1))
                    last.then_inc(d2.out, 1)

                chunks(pe, chunk)

            @block.scalar
            def _(act):
                act.sem_inc(d2.copied, 2)
                act.wait_ge(w2_turned, 1)
                act.activation(wt[:, 0:2, :].rearrange("p k n -> p (k n)"), bank[3][:, 0:2 * F], ACT.Copy).then_inc(w2_copied, 1)
                chunks(act, lambda c, n: copy_two(act, d2, c, n))

            @block.vector
            def _(dve):
                dve.sem_inc(d2.added, 1)

                def chunk(c, n):
                    stage_means(dve, d2, c, n)
                    xs = x_sb[:, tiles(c, n), :]
                    dve.tensor_tensor(xs, xs, bs_bc.broadcast_to([P, n, F]), ALU.add).then_inc(x_chain, 1)
                    dve.wait_ge(x_chain, c + 1)
                    dve.wait_ge(d2.out, c + 2)
                    dve.tensor_tensor(xs, xs, bank[2][:, 0:n * F].rearrange("p (t f) -> p t f", f=F), ALU.add).then_inc(d2.added, 1)

                chunks(dve, chunk)

        recycle_semaphores()
        layer_norm("3")

        xrow = acc[:, 0:NT * RW].rearrange("p (t h w) -> p t h w", t=NT, h=HEADS)
        node_tab = sb("node_tab", [P, NT, 2 * HEADS])
        d3 = Dense("l3d", 1)
        w3_in, t_chain, t_out, ones_set = sem("l3_weights_in"), sem("l3_chain"), sem("l3_table_out"), sem("l3_ones")
        prod = gelu_t
        as_bc = av[:, :, 0:HO].rearrange("p h (a o) -> p a h o", a=1)
        ad_bc = av[:, :, HO:2 * HO].rearrange("p h (a o) -> p a h o", a=1)
        with nc.Block() as block:
            @block.sync
            def _(sp):
                sp.dma_start(wt[:, 0, :].rearrange("p (h o) -> p h o", h=HEADS), Wgat.rearrange("h i o -> i h o")).then_inc(w3_in, 16)
                sp.wait_ge(t_chain, 5 * (NC + NT - NC * CT))
                sp.wait_ge(ones_set, 1)
                sp.dma_start(xt_rows.rearrange("(t p) w -> p t w", p=P), xrow.rearrange("p t h w -> p t (h w)")).then_inc(t_out, 16)
                sp.wait_ge(t_out, 16)

            @block.gpsimd
            def _(pool):
                pool.memset(xrow[:, :, :, HO:HO + 1].rearrange("p t h w -> p (t h) w"), 1.0).then_inc(ones_set, 1)

                def copy_in(c, n):
                    pool.wait_ge(d3.turned, c + 1)
                    pool.tensor_copy(stage[:, 0:n, 0, :], h_sb[:, tiles(c, n), :]).then_inc(d3.copied_in, 1)

                chunks(pool, copy_in)

            @block.tensor
            def _(pe):
                pe.sem_inc(d3.turned, 1)
                pe.sem_inc(d3.out, 1)
                pe.wait_ge(w3_in, 16)

                def chunk(c, n):
                    pe.wait_ge(d3.copied_in, c + 1)
                    pe.wait_ge(d3.copied, c + 1)
                    for i in range(n):
                        last = pe.transpose(bank[0][:, i * P:(i + 1) * P], stage[:, i, 0, :], ident[:, :])
                    last.then_inc(d3.turned, 1)
                    pe.wait_ge(d3.copied, c + 2)
                    pe.wait_ge(t_chain, 5 * c + 1)
                    for i in range(n):
                        last = pe.matmul(bank[2][:, i * F:(i + 1) * F], turn2[:, 0, i * P:(i + 1) * P], wt[:, 0, :], start=True, stop=True)
                    last.then_inc(d3.out, 1)

                chunks(pe, chunk)

            @block.scalar
            def _(act):
                act.sem_inc(d3.copied, 1)

                def chunk(c, n):
                    act.wait_ge(d3.out, c + 1)
                    act.wait_ge(d3.turned, c + 2)
                    act.activation(turn2[:, 0, 0:n * P], bank[0][:, 0:n * P], ACT.Copy).then_inc(d3.copied, 1)

                chunks(act, chunk)

            @block.vector
            def _(dve):
                dve.memset(node_tab[:, :, HEADS:2 * HEADS], -BIG).then_inc(t_chain, 1)

                def chunk(c, n):
                    y = bank[2][:, 0:n * F].rearrange("p (t h o) -> p t h o", h=HEADS, o=HO)
                    pr = prod[:, 0:n * F].rearrange("p (t h o) -> p t h o", h=HEADS, o=HO)
                    dve.wait_ge(d3.out, c + 2)
                    dve.wait_ge(t_chain, 5 * c + 1)
                    dve.tensor_scalar(xrow[:, tiles(c, n), :, 0:HO], y, 1.0, None, ALU.mult).then_inc(t_chain, 1)
                    dve.tensor_tensor(pr, y, as_bc.broadcast_to([P, n, HEADS, HO]), ALU.mult).then_inc(t_chain, 1)
                    dve.wait_ge(t_chain, 5 * c + 3)
                    dve.tensor_reduce(xrow[:, tiles(c, n), :, HO + 1], pr, AX.X, ALU.add).then_inc(t_chain, 1)
                    dve.wait_ge(t_chain, 5 * c + 4)
                    dve.tensor_tensor(pr, y, ad_bc.broadcast_to([P, n, HEADS, HO]), ALU.mult).then_inc(t_chain, 1)
                    dve.wait_ge(t_chain, 5 * c + 5)
                    dve.tensor_reduce(node_tab[:, tiles(c, n), 0:HEADS], pr, AX.X, ALU.add).then_inc(t_chain, 1)

                chunks(dve, chunk)

        acc3 = acc[:, 0:NT * HEADS * HW].rearrange("p (t h w) -> p t h w", t=NT, h=HEADS)
        GH = G * HEADS
        pos = [OFF3]

        def small_buf(*shape):
            n = int(np.prod(shape))
            v = work[:, pos[0]:pos[0] + n]
            pos[0] += n
            names = "abc"[0:len(shape)]
            spec = " ".join(names)
            return v.rearrange(f"p ({spec}) -> p {spec}", **{k: d for k, d in zip(names[:-1], shape[:-1])})

        weighted = small_buf(D, GH, HW)
        src_score, max_one = small_buf(D, GH), small_buf(D, G, HEADS + 1)
        node_now, absent, tile_max = small_buf(D, 2 * HEADS), small_buf(D, G), small_buf(D, G, HEADS)
        m_max, m_sum, m_relu, m_drop, alpha = (small_buf(D, HEADS) for _ in range(5))
        e_sum, e_relu, e_diff, weight = (small_buf(D, GH) for _ in range(4))
        ones_row = small_buf(G * NSP)
        onehot_t = lastmax
        rows3 = edge_buf.rearrange("p u g (h w) -> p u (g h) w", w=HW + 1)
        hotT = bank[0][:, 0:W]
        scoreT = bank[1][0:GH, 0:P]
        maxT = bank[2][:, 0:GH]
        nodeM = [bank[3 + q][:, 0:G * (HEADS + 1)].rearrange("p (g k) -> p g k", g=G) for q in range(2)]
        edgeV = bank[5][:, 0:G * 2 * HEADS].rearrange("p (g k) -> p g k", g=G)
        total = [bank[6][:, 0:HEADS * HW], bank[7][:, 0:HEADS * HW]]
        got3 = [sem(f"l3_rows_in{j}") for j in range(U)]
        pen3_in = [sem(f"l3_pen_in{j}") for j in range(D)]
        (idx3, rows_used, scored, hot3, score_turned, hot_turned, hot_copied, last_made, scan3, back3, max_in, node_max,
         m_chain, m_ready, m_dropped, alpha_made, edge_values, e_chain, e_ready, weights_made, w_ready, total_ready,
         acc_chain, flags, set3) = (sem(f"l3_{s}") for s in (
             "indices", "rows_used", "scored", "one_hot", "scores_turned", "one_hot_turned", "one_hot_copied", "last_made",
             "scanned", "max_turned_back", "max_in", "node_max", "m_chain", "m_ready", "m_dropped", "alpha_made",
             "edge_values", "e_chain", "e_ready", "weights_made", "weighted", "total", "acc_chain", "flags", "set"))
        go3, go_pe, act_go3 = sem("l3_go"), sem("l3_go_pe"), sem("l3_act_go")
        with nc.Block() as block:
            @block.sync
            def _(sp):
                sp.wait_ge(flags, 1)
                sp.dma_start(last_flag[P - 1:P, :, :].rearrange("p g s -> p (g s)"), ones_row[0:1, :]).then_inc(set3, 16)
                with sp.Fori(0, IT) as t:
                    for j in range(U):
                        s = t * U + j
                        sp.wait_ge(scan3, s + 1)
                        for g in range(G):
                            sp.dma_start(pen_buf[g * HEADS:(g + 1) * HEADS, j % D, 0:P],
                                         pen_rows[bass.ds(s, 1), g * P:(g + 1) * P].broadcast_to([HEADS, P])).then_inc(pen3_in[j % D], 16)

            @block.gpsimd
            def _(pool):
                gather(pool, xt_rows, RW, got3, idx3, go3)

            @block.tensor
            def _(pe):
                def turn(t, j, _):
                    s = t * U + j
                    pe.wait_ge(scored, s + 1)
                    pe.transpose(scoreT, src_score[:, j % D, :], ident[:, :]).then_inc(score_turned, 1)
                    pe.wait_ge(hot3, s + 1)
                    pe.wait_ge(hot_copied, s + 1)
                    for g in range(G):
                        last = pe.transpose(hotT[:, g * P:(g + 1) * P], onehot[:, j % D, g, :], ident[:, :])
                    last.then_inc(hot_turned, 1)
                    pe.wait_ge(scan3, s + D + 1)
                    pe.sem_inc(go_pe, 1)
                    pe.transpose(maxT, scan_buf[0:GH, j % D, 0:P], ident[0:GH, 0:GH]).then_inc(back3, 1)
                    pe.wait_ge(max_in, s + 1)
                    pe.wait_ge(last_made, s + 1)
                    for g in range(G):
                        last = pe.matmul(nodeM[j % 2][:, g, :], onehot_last[:, j % D, g, :], max_one[:, j % D, g, :], start=True, stop=True)
                    last.then_inc(node_max, 1)

                def to_edges(t, j, _):
                    s = t * U + j
                    pe.wait_ge(m_ready, s + 1)
                    pe.wait_ge(hot_copied, s + 2)
                    for g in range(G):
                        last = pe.matmul(edgeV[:, g, :], onehot_t[:, j % D, g, :], node_now[:, j % D, :], start=True, stop=True)
                    last.then_inc(edge_values, 1)

                def to_nodes(t, j, _):
                    s = t * U + j
                    pe.wait_ge(w_ready, s + 1)
                    for g in range(G):
                        last = pe.matmul(total[j % 2], onehot[:, j % D, g, :],
                                         weighted[:, j % D, g * HEADS:(g + 1) * HEADS, :].rearrange("p h w -> p (h w)"),
                                         start=(g == 0), stop=(g == G - 1))
                    last.then_inc(total_ready, 1)

                run_steps(pe, [(turn, 0), (to_edges, 1), (to_nodes, 2)])

            @block.scalar
            def _(act):
                act.sem_inc(hot_copied, 1)
                act.wait_ge(set3, 16)
                act.wait_ge(flags, 2)

                def copies(t, j, _):
                    s = t * U + j
                    act.wait_ge(hot_turned, s + 1)
                    act.activation(onehot_t[:, j % D, :, :], hotT.rearrange("p (g n) -> p g n", g=G), ACT.Copy).then_inc(hot_copied, 1)
                    for g in range(G):
                        last = act.activation(onehot_last[:, j % D, g, :], onehot[:, j % D, g, :], ACT.Copy, scale=last_flag[:, g, bass.ds(s, 1)])
                    last.then_inc(last_made, 1)

                def weights(t, j, _):
                    s = t * U + j
                    act.wait_ge(e_ready, s + 1)
                    act.activation(weight[:, j % D, :], e_diff[:, j % D, :], ACT.Exp).then_inc(weights_made, 1)

                def maxima(t, j, _):
                    s = t * U + j
                    act.wait_ge(back3, s + 1)
                    act.activation(max_one[:, j % D, :, 0:HEADS], maxT.rearrange("p (g h) -> p g h", g=G), ACT.Copy).then_inc(max_in, 1)

                def rescale(t, j, _):
                    s = t * U + j
                    act.wait_ge(m_dropped, s + 1)
                    act.activation(alpha[:, j % D, :], m_drop[:, j % D, :], ACT.Exp).then_inc(alpha_made, 1)

                for j in range(U // 2):
                    place_indices(act, 0, j, rows_used, idx3, act_go3)

                def indices(t, j, _):
                    if isinstance(t, int):
                        t, j = t + (j + U // 2) // U, (j + U // 2) % U
                        if t >= IT:
                            return
                        place_indices(act, t, j, rows_used, idx3, act_go3)
                    else:
                        place_indices(act, t + (j + U // 2) // U, (j + U // 2) % U, rows_used, idx3, act_go3)

                run_steps(act, [(copies, 0), (weights, 2), (maxima, 0), (rescale, 1), (indices, 0)])

            @block.vector
            def _(dve):
                dve.sem_inc(rows_used, U)
                dve.sem_inc(scan3, D)
                dve.memset(ones_row[0:1, :], 1.0).then_inc(flags, 1)
                dve.memset(max_one[:, :, :, HEADS:HEADS + 1], 1.0).then_inc(flags, 1)
                dve.memset(acc[:, 0:NT * HEADS * HW], 0.0).then_inc(flags, 1)
                dve.wait_ge(flags, 3)

                def scores(t, j, _):
                    s = t * U + j
                    dve.wait_ge(got3[j], 16 * G * (t + 1))
                    dve.tensor_tensor(src_score[:, j % D, :].rearrange("p (g h) -> p g h", g=G),
                                      edge_buf[:, j, :, :].rearrange("p g (h w) -> p g h w", w=HW + 1)[:, :, :, HW],
                                      score_e[:, :, :, bass.ds(s, 1)].rearrange("p h g a -> p g (h a)"), ALU.add).then_inc(scored, 1)
                    for g in range(G):
                        last = dve.tensor_scalar(onehot[:, j % D, g, :], iota_n[:, :], node_key[:, g, bass.ds(s, 1)], None, ALU.is_equal)
                    last.then_inc(hot3, 1)

                def exponents(t, j, _):
                    s = t * U + j
                    dve.wait_ge(edge_values, s + 1)
                    sc = src_score[:, j % D, :].rearrange("p (g h) -> p g h", g=G)
                    dve.tensor_tensor(e_sum[:, j % D, :].rearrange("p (g h) -> p g h", g=G), sc, edgeV[:, :, 0:HEADS],
                                      ALU.add).then_inc(e_chain, 1)
                    dve.wait_ge(e_chain, 2 * s + 1)
                    dve.scalar_tensor_tensor(out=e_relu[:, j % D, :], in0=e_sum[:, j % D, :], scalar=0.2, in1=e_sum[:, j % D, :],
                                             op0=ALU.mult, op1=ALU.max).then_inc(e_chain, 1)
                    dve.wait_ge(e_chain, 2 * s + 2)
                    dve.tensor_tensor(e_diff[:, j % D, :].rearrange("p (g h) -> p g h", g=G),
                                      e_relu[:, j % D, :].rearrange("p (g h) -> p g h", g=G), edgeV[:, :, HEADS:2 * HEADS],
                                      ALU.subtract).then_inc(e_ready, 1)

                def scan(t, j, _):
                    s = t * U + j
                    dve.wait_ge(score_turned, s + 1)
                    dve.wait_ge(pen3_in[j % D], 16 * G * turn_of(t, j))
                    dve.tensor_tensor_scan(scan_buf[0:GH, j % D, 0:P], pen_buf[0:GH, j % D, 0:P], scoreT, -PEN,
                                           ALU.add, ALU.max).then_inc(scan3, 1)

                def node_maxima(t, j, tile):
                    s = t * U + j
                    K = 7
                    tab = node_tab[:, bass.ds(tile, 1), :].rearrange("p a k -> p (a k)")
                    dve.wait_ge(node_max, s + 1)
                    dve.tensor_scalar(absent[:, j % D, :], nodeM[j % 2][:, :, HEADS], BIG, -BIG, ALU.mult, ALU.add).then_inc(m_chain, 1)
                    dve.wait_ge(m_chain, K * s + 1)
                    dve.tensor_tensor(tile_max[:, j % D, :, :], nodeM[j % 2][:, :, 0:HEADS],
                                      absent[:, j % D, :].rearrange("p (g a) -> p g a", a=1).broadcast_to([P, G, HEADS]), ALU.add).then_inc(m_chain, 1)
                    dve.wait_ge(m_chain, K * s + 2)
                    dve.tensor_tensor(m_max[:, j % D, :], tile_max[:, j % D, 0, :], tile_max[:, j % D, 1, :], ALU.max).then_inc(m_chain, 1)
                    dve.wait_ge(m_chain, K * s + 3)
                    dve.tensor_tensor(m_sum[:, j % D, :], m_max[:, j % D, :], tab[:, 0:HEADS], ALU.add).then_inc(m_chain, 1)
                    dve.wait_ge(m_chain, K * s + 4)
                    dve.scalar_tensor_tensor(out=m_relu[:, j % D, :], in0=m_sum[:, j % D, :], scalar=0.2, in1=m_sum[:, j % D, :],
                                             op0=ALU.mult, op1=ALU.max).then_inc(m_chain, 1)
                    dve.wait_ge(m_chain, K * s + 5)
                    if not (isinstance(t, int) and s == 0):
                        dve.wait_ge(m_ready, s)
                    dve.tensor_tensor(node_now[:, j % D, HEADS:2 * HEADS], m_relu[:, j % D, :], tab[:, HEADS:2 * HEADS], ALU.max).then_inc(m_chain, 1)
                    dve.tensor_copy(node_now[:, j % D, 0:HEADS], tab[:, 0:HEADS]).then_inc(m_chain, 1)
                    dve.wait_ge(m_chain, K * s + 7)
                    dve.tensor_tensor(m_drop[:, j % D, :], tab[:, HEADS:2 * HEADS], node_now[:, j % D, HEADS:2 * HEADS],
                                      ALU.subtract).then_inc(m_dropped, 1)
                    dve.wait_ge(m_dropped, s + 1)
                    dve.tensor_scalar(tab[:, HEADS:2 * HEADS], node_now[:, j % D, HEADS:2 * HEADS], 1.0, None, ALU.mult).then_inc(m_ready, 1)

                def weigh(t, j, _):
                    s = t * U + j
                    dve.wait_ge(weights_made, s + 1)
                    dve.scalar_tensor_tensor(out=weighted[:, j % D, :, :],
                                             in0=weight[:, j % D, :].rearrange("p (k a) -> p k a", a=1).broadcast_to([P, GH, HW]),
                                             scalar=1.0, in1=rows3[:, j, :, 0:HW], op0=ALU.min, op1=ALU.mult).then_inc(w_ready, 1)
                    dve.wait_ge(w_ready, s + 1)
                    dve.sem_inc(rows_used, 1)

                def add(t, j, tile):
                    s = t * U + j
                    row = acc3[:, bass.ds(tile, 1), :, :].rearrange("p a h w -> p (a h) w")
                    dve.wait_ge(alpha_made, s + 1)
                    dve.wait_ge(total_ready, s + 1)
                    if not (isinstance(t, int) and s == 0):
                        dve.wait_ge(acc_chain, 2 * s)
                    dve.scalar_tensor_tensor(out=row, in0=alpha[:, j % D, :].rearrange("p (h a) -> p h a", a=1).broadcast_to([P, HEADS, HW]),
                                             scalar=1.0, in1=row, op0=ALU.min, op1=ALU.mult).then_inc(acc_chain, 1)
                    dve.wait_ge(acc_chain, 2 * s + 1)
                    dve.tensor_tensor(row, row, total[j % 2].rearrange("p (h w) -> p h w", h=HEADS), ALU.add).then_inc(acc_chain, 1)

                run_steps(dve, [(scores, 0), (exponents, 2), (scan, 0), (node_maxima, 1), (weigh, 2), (add, 3)],
                          before=lambda t: tiles_of_steps(t, [1, 3]))

        f_chain, f_out = sem("final_chain"), sem("final_out")
        inv = stats[:, :, 0:HEADS]
        with nc.Block() as block:
            @block.vector
            def _(dve):
                step = Count(f_chain)

                def link(ins):
                    dve.wait_ge(f_chain, step.inc(ins))

                link(dve.tensor_scalar(inv, acc3[:, :, :, HO], 1e-10, None, ALU.add))
                link(dve.reciprocal(inv, inv))
                half = NT // 2
                for a, b in ((0, half), (half, NT)):
                    xs = x_sb[:, a:b, :].rearrange("p t (h o) -> p t h o", h=HEADS)
                    hs = h_sb[:, a:b, :].rearrange("p t (h o) -> p t h o", h=HEADS)
                    link(dve.tensor_tensor(hs, acc3[:, a:b, :, 0:HO],
                                           inv[:, a:b, :].rearrange("p t (h a) -> p t h a", a=1).broadcast_to([P, b - a, HEADS, HO]), ALU.mult))
                    link(dve.tensor_tensor(xs, xs, hs, ALU.add))

            @block.sync
            def _(sp):
                half = NT // 2
                sp.wait_ge(f_chain, 4)
                sp.dma_start(out[0:half * P, :].rearrange("(t p) f -> p t f", p=P), x_sb[:, 0:half, :]).then_inc(f_out, 16)
                sp.wait_ge(f_chain, 6)
                sp.dma_start(out[half * P:(NT - 1) * P, :].rearrange("(t p) f -> p t f", p=P), x_sb[:, half:NT - 1, :]).then_inc(f_out, 16)
                sp.dma_start(out[(NT - 1) * P:N, :], x_sb[0:LAST, NT - 1, :]).then_inc(f_out, 16)
                sp.wait_ge(f_out, 48)


_INS = ['x', 'src', 'dst', 'edge_attr_128', 'edge_attr_8', 'L0_gnn_u', 'L0_gnn_W1', 'L0_gnn_b1', 'L0_gnn_W2', 'L0_gnn_b2',
        'L1_gnn_W_l', 'L1_gnn_b_l', 'L1_gnn_W_r', 'L1_gnn_gn_weight', 'L1_gnn_gn_bias', 'L1_gnn_gn_mean_scale',
        'L2_gnn_W', 'L2_gnn_b', 'L3_gnn_W', 'L3_gnn_a']
_OUTS = [((6250, 128), 'float32')]


def kernel(**inputs):
    import numpy as _np
    import concourse.bacc as _bacc
    from concourse import mybir as _mybir
    from concourse.bass_utils import run_bass_kernel_spmd as _run

    nc = _bacc.Bacc("TRN2", target_bir_lowering=False, num_devices=1)
    arrays, args = {}, []
    for name in _INS:
        a = _np.ascontiguousarray(inputs[name])
        arrays[f"in_{name}_dram"] = a
        args.append(nc.dram_tensor(f"in_{name}_dram", a.shape, _mybir.dt.from_np(a.dtype), kind="ExternalInput").ap())
    for i, (shape, dtype) in enumerate(_OUTS):
        dt = _mybir.dt.from_np(_np.dtype(dtype))
        args.append(nc.dram_tensor(f"out_{i}_dram", shape, dt, kind="ExternalOutput").ap())
    gnn_program(nc, *args)
    r = _run(nc, [arrays], core_ids=[0])
    got = tuple(r.results[0][f"out_{i}_dram"] for i in range(len(_OUTS)))
    return got[0]
```

```python
from contextlib import ExitStack

import numpy as np

import concourse.bass as bass
from concourse import mybir

F32 = mybir.dt.float32
BF16 = mybir.dt.bfloat16
I32 = mybir.dt.int32
ALU = mybir.AluOpType
ACT = mybir.ActivationFunctionType
AX = mybir.AxisListType
DVE_ENGINE = (mybir.EngineType.DVE,)
SP_ENGINE = (mybir.EngineType.SP,)

P = 128
N, F = 6250, 128
E = 200000
HID = 1024
KH = HID // P
HEADS, HO, EA = 4, 32, 8
HW = HO + 1
RW = HEADS * (HW + 1)
NT = -(-N // P)
LAST = N - (NT - 1) * P
CT = 4
NC = NT // CT
FAR = 1.0e6
PEN = 3.0e38
BIG = 1.0e38
EPS = 1e-5


class Plan:

    def __init__(self, G, U, D):
        self.G, self.U, self.D = G, U, D
        self.W = G * P
        self.FULL = E // self.W
        self.NG = -(-E // self.W)
        self.DUP = self.NG * self.W - E
        self.NS = self.NG + NT - 1
        self.IT = -(-self.NS // U)
        self.STEPS = self.IT * U
        self.NB = -(-self.STEPS // P)


WIDE = Plan(4, 4, 4)
DEEP = Plan(4, 8, 4)
FINE = Plan(1, 8, 4)


assert DEEP.STEPS == WIDE.STEPS
PAD = 8
AHEAD = 3


class Count:

    def __init__(self, sem):
        self.sem, self.n = sem, 0

    def inc(self, ins, by=1):
        ins.then_inc(self.sem, by)
        self.n += by
        return self.n


def gnn_program(nc, x, src, dst, edge_attr, edge_attr8, u0, W1, b1, W2, b2, Wl, bl, Wr, gw, gb, gms,
                Wsage, bsage, Wgat, agat, out):
    ctx = ExitStack()
    with ctx:
        G, U, D, W, NG, IT, STEPS, NB = (WIDE.G, WIDE.U, WIDE.D, WIDE.W, WIDE.NG, WIDE.IT, WIDE.STEPS, WIDE.NB)

        def sb(name, shape, dt=F32):
            return ctx.enter_context(nc.sbuf_tensor(name, shape, dt))

        used_sems = []

        def sem(name):
            used_sems.append(nc.alloc_semaphore(name=name))
            return used_sems[-1]


        def recycle_semaphores():
            nc.clear_and_free_semaphores(used_sems)
            used_sems.clear()
            nc.all_engine_barrier()

        def dram(name, shape, dt=F32):
            return nc.dram_tensor(name, shape, dt, kind="Internal").ap()

        src_rows = dram("src_rows", [NG, W], I32)
        dst_rows = dram("dst_rows", [NG, W], I32)
        prev_rows = dram("prev_rows", [NG, W], I32)
        next_rows = dram("next_rows", [NG, W], I32)
        src_fine = dram("src_fine", [FINE.NG, FINE.W], I32)
        dst_fine = dram("dst_fine", [FINE.NG, FINE.W], I32)
        ea8_rows = dram("ea8_rows", [NG, W * EA])
        pen_rows = dram("pen_rows", [NB * P, W], BF16)
        h_rows = dram("h_rows", [NT * P, F])
        xt_rows = dram("xt_rows", [NT * P, RW])

        x_sb = sb("x_sb", [P, NT, F])
        h_sb = sb("h_sb", [P, NT, F])
        ident = sb("ident", [P, P])
        iota_n = sb("iota_n", [P, P])
        node_key = sb("node_key", [P, G, STEPS])
        last_flag = sb("last_flag", [P, G, STEPS])
        src_idx = sb("src_idx", [P, G, STEPS + AHEAD], I32)
        nt_row = sb("nt_row", [1, 2 * PAD + STEPS], I32)
        base_row = sb("base_row", [1, STEPS], I32)
        rdeg = sb("rdeg", [P, NT])
        bias_bc = sb("bias_bc", [P, 2, F])
        small = sb("small", [P, 64])
        a_bc = sb("a_bc", [P, HEADS * (2 * HO + EA)])
        eg_col = sb("eg_col", [P, NB], I32)
        eg_fine = sb("eg_fine", [P, FINE.NB], I32)
        idx_now = sb("idx_now", [P, max(DEEP.G * DEEP.U, FINE.G * FINE.U)], I32)
        acc = sb("acc", [P, NT * (2 * F + 1)])

        def carve(region):
            at = [0]

            def take(*shape):
                n = int(np.prod(shape))
                v = region[:, at[0]:at[0] + n]
                at[0] += n
                names = "abcd"[0:len(shape)]
                return v.rearrange(f"p ({' '.join(names)}) -> p {' '.join(names)}", **dict(zip(names[:-1], shape[:-1])))
            return take

        step_mem = sb("step_mem", [P, DEEP.U * G * RW + D * W // 2 + 6 * W])
        take = carve(step_mem)
        edge_buf = take(U, G, RW)
        onehot = take(D, G, P)
        lastmax = take(2, G, P)
        scan_buf = take(2, W)
        pen_buf = take(D, W // 2).bitcast(BF16)
        take = carve(step_mem)
        CW = CT * P
        stage = take(CT, 4, F)
        gelu_t = take(CW)
        turn2 = take(2, CW)
        wt = take(2, F)
        stats = take(NT, 6)
        mv = take(NT, 2)
        veps, std, rstd, nmr, deg = (take(NT) for _ in range(5))
        WORK = 4 * HID + KH * F + 4 * CW + KH * CW
        work = sb("work", [P, WORK])
        score_e = carve(work)(HEADS, G, STEPS)
        take = carve(work)
        key_fine = take(FINE.G, FINE.STEPS)
        src_idx_fine = take(FINE.G, FINE.STEPS).bitcast(I32)
        nt_row_fine = take(2 * PAD + FINE.STEPS).bitcast(I32)

        bank = [ctx.enter_context(nc.psum_tensor(f"bank{i}", [P, 512], F32)) for i in range(8)]

        def sv(c):
            return small[:, c:c + 1]

        def flat(a):
            return a.rearrange("a b -> (a b)")

        def step_tables(tag, plan, take_raw, take_tmp, eg_idx, key, index, tile_row, base=None, flag=None, first=False):
            G, U, W, NG, FULL, DUP, NB, STEPS = (plan.G, plan.U, plan.W, plan.NG, plan.FULL, plan.DUP, plan.NB, plan.STEPS)
            NBP, K = NB * P, 4 if first else 2
            rows = (dst_rows, src_rows, prev_rows, next_rows) if first else (dst_fine, src_fine)
            raw = take_raw(K, NB, W).bitcast(I32)
            keyf, srcf = take_tmp(NB, W), take_tmp(NB, W)
            if first:
                eqf, lastf = take_tmp(NB, W), take_tmp(NB, W)
                pen_w = take_raw(NB, W // 2).bitcast(BF16)
            srow, ind, ntf = take_raw(NBP), take_raw(NBP), take_raw(NBP)
            befr = take_raw(NBP) if first else None
            less = take_tmp(NB, NT - 1)
            tgrid, scol, ldf, ntc, egf, kill1, koff = take_tmp(NT - 1), *(take_tmp(NB) for _ in range(6))
            ldi, onesk, thr, consts_i = take_tmp(NB).bitcast(I32), take_tmp(1), take_tmp(1), take_tmp(2).bitcast(I32)
            RB = 4 if NBP > 1024 else 2
            RC = NBP // RB

            names = ("rows_in", "small_in", "consts", "iotas", "ident_zero", "ident_made", "before_mm", "col_mm", "row_mm",
                     "t_dve", "eg_ready", "raw_in", "keys_ready", "turned", "turned_used", "pen_out", "fine_in")
            (rows_in, small_in, consts, iotas, ident_zero, ident_made, before_mm, col_mm, row_mm,
             t_dve, eg_ready, raw_in, keys_ready, turned, turned_used, pen_out, fine_in) = (sem(f"{tag}_{n}") for n in names)
            kinds = 3 if first else 2

            def split_copy(sp, to, frm, parts, done=rows_in):
                sp.dma_start(to.rearrange("(a b) -> a b", a=parts), frm.rearrange("(a b) -> a b", a=parts)).then_inc(done, 16)

            with nc.Block() as block:
                @block.sync
                def _(sp):
                    with nc.allow_non_contiguous_dma(reason="one last destination of each group"):
                        for c in range(-(-FULL // P)):
                            n = min(P, FULL - c * P)
                            if c == 0:
                                sp.wait_ge(consts, 1)
                            sp.dma_start(ldi[0:n, c:c + 1],
                                         dst[c * P * W:(c * P + n) * W].rearrange("(p w) -> p w", w=W)[:, W - 1:W]
                                         ).then_inc(small_in, 16)
                    if not first:
                        return
                    cut = FULL * W
                    for to, frm in ((dst_rows, dst), (src_rows, src)):
                        split_copy(sp, flat(to)[0:cut], frm[0:cut], 10)
                        sp.dma_start(to[FULL:NG, :], frm[E - W:E].rearrange("(a b) -> a b", a=1)).then_inc(rows_in, 16)
                    split_copy(sp, flat(prev_rows)[W:cut], dst[W - 1:cut - 1], FULL - 1)
                    sp.dma_start(prev_rows[0:1, 1:W], dst[0:W - 1].rearrange("(a b) -> a b", a=1)).then_inc(rows_in, 16)
                    sp.dma_start(prev_rows[FULL:NG, :], dst[E - W - 1:E - 1].rearrange("(a b) -> a b", a=1)).then_inc(rows_in, 16)
                    split_copy(sp, flat(next_rows)[0:cut], dst[1:cut + 1], 10)
                    sp.dma_start(next_rows[FULL:NG, 0:W - 1], dst[E - W + 1:E].rearrange("(a b) -> a b", a=1)).then_inc(rows_in, 16)
                    sp.wait_ge(consts, 3)
                    sp.dma_start(prev_rows[0:1, 0:1], consts_i[0:1, 0:1]).then_inc(rows_in, 16)
                    sp.dma_start(next_rows[FULL:NG, W - 1:W], consts_i[0:1, 1:2]).then_inc(rows_in, 16)
                    fcut = FINE.FULL * FINE.W
                    for to, frm in ((dst_fine, dst), (src_fine, src)):
                        split_copy(sp, flat(to)[0:fcut], frm[0:fcut], 11, fine_in)
                        sp.dma_start(to[FINE.FULL:FINE.NG, :], frm[E - FINE.W:E].rearrange("(a b) -> a b", a=1)).then_inc(fine_in, 16)
                    for a in range(10):
                        n = FULL // 10
                        sp.dma_start(ea8_rows[a * n:(a + 1) * n, :],
                                     edge_attr8[a * n * W:(a + 1) * n * W, :].rearrange("(a w) k -> a (w k)", w=W)).then_inc(fine_in, 16)
                    sp.dma_start(ea8_rows[FULL:NG, :], edge_attr8[E - W:E, :].rearrange("(a w) k -> a (w k)", w=W)).then_inc(fine_in, 16)
                    sp.wait_ge(keys_ready, 1)
                    sp.dma_start(pen_rows.rearrange("(c p) w -> p c w", p=P), pen_w).then_inc(pen_out, 16)
                    sp.wait_ge(pen_out, 16)
                    sp.wait_ge(fine_in, 16 * 15)

                @block.gpsimd
                def _(pool):
                    pool.memset(ldi, 2 ** 30).then_inc(consts, 1)
                    pool.memset(consts_i[:, 0:1], -1).then_inc(consts, 1)
                    pool.memset(consts_i[:, 1:2], 2 ** 20).then_inc(consts, 1)
                    pool.iota(tgrid, [[P, NT - 1]], base=P, channel_multiplier=0,
                              allow_small_or_imprecise_dtypes=True).then_inc(iotas, 1)
                    pool.iota(srow, [[1, NBP]], base=0, channel_multiplier=0,
                              allow_small_or_imprecise_dtypes=True).then_inc(iotas, 1)
                    pool.iota(scol, [[P, NB]], base=0, channel_multiplier=1,
                              allow_small_or_imprecise_dtypes=True).then_inc(iotas, 1)
                    pool.iota(thr, [[0, 1]], base=1, channel_multiplier=1,
                              allow_small_or_imprecise_dtypes=True).then_inc(iotas, 1)
                    pool.memset(onesk, 1.0).then_inc(iotas, 1)
                    if first:
                        pool.memset(index[:, :, STEPS:STEPS + AHEAD], 0).then_inc(iotas, 1)
                        pool.iota(iota_n[:, :], [[1, P]], base=0, channel_multiplier=0,
                                  allow_small_or_imprecise_dtypes=True).then_inc(ident_zero, 1)
                        pool.memset(ident[:, :], 0.0).then_inc(ident_zero, 1)
                        pool.wait_ge(ident_zero, 2)
                        pool.affine_select(out=ident[:, :], in_=ident[:, :], compare_op=ALU.not_equal, fill=1.0,
                                           base=0, pattern=[[-1, P]], channel_multiplier=1).then_inc(ident_made, 1)
                        pool.wait_ge(rows_in, 16 * 11)
                    pool.wait_ge(eg_ready, 1)
                    for c in range(NB):
                        for k in range(K):
                            pool.indirect_dma_start(raw[:, k, c, :], None, rows[k][:, :],
                                                    bass.IndirectOffsetOnAxis(ap=eg_idx[:, c:c + 1], axis=0)
                                                    ).then_inc(raw_in, 16)

                @block.tensor
                def _(pe):
                    pe.wait_ge(t_dve, 1 + NB)
                    for c in range(NB):
                        last = pe.matmul(bank[0][0:NT - 1, 0:1], less[:, c, 0:NT - 1], onesk, start=(c == 0), stop=(c == NB - 1))
                    last.then_inc(before_mm, 1)
                    pe.wait_ge(t_dve, 3 + NB)
                    for c in range(NB):
                        last = pe.matmul(bank[1][:, c:c + 1], ind[0:NT - 1, c * P:(c + 1) * P], onesk[0:NT - 1, :],
                                         start=True, stop=True)
                    last.then_inc(col_mm, 1)
                    for i in range(RB):
                        last = pe.matmul(bank[2 + i][0:1, 0:RC], onesk[0:NT - 1, :],
                                         ind[0:NT - 1, i * RC:(i + 1) * RC], start=True, stop=True)
                    last.then_inc(row_mm, 1)
                    if first:
                        pe.wait_ge(ident_made, 1)
                    pe.wait_ge(keys_ready, 1)
                    for c in range(NB):
                        for k, table in enumerate((keyf, srcf, lastf) if first else (keyf, srcf)):
                            q = kinds * c + k
                            if q >= 6:
                                pe.wait_ge(turned_used, q - 5)
                            for g in range(G):
                                last = pe.transpose(bank[q % 6][:, g * P:(g + 1) * P], table[:, c, g * P:(g + 1) * P], ident[:, :])
                            last.then_inc(turned, 1)

                @block.vector
                def _(dve):
                    step = Count(t_dve)

                    def link(ins):
                        dve.wait_ge(t_dve, step.inc(ins))

                    dve.wait_ge(iotas, 6 if first else 5)
                    dve.wait_ge(small_in, 16 * -(-FULL // P))
                    link(dve.tensor_copy(ldf, ldi))
                    for c in range(NB):
                        step.inc(dve.tensor_scalar(less[:, c, 0:NT - 1], tgrid, ldf[:, c:c + 1], None, ALU.is_gt))
                    dve.wait_ge(before_mm, 1)
                    link(dve.tensor_tensor(thr[0:NT - 1, :], bank[0][0:NT - 1, 0:1], thr[0:NT - 1, :], ALU.add))
                    step.inc(dve.tensor_scalar(ind[0:NT - 1, :], srow[0:NT - 1, :], thr[0:NT - 1, :], None, ALU.is_ge))
                    dve.wait_ge(col_mm, 1)
                    link(dve.tensor_copy(ntc, bank[1][:, 0:NB]))
                    link(dve.tensor_tensor(egf, scol, ntc, ALU.subtract))
                    dve.tensor_scalar(eg_idx[:, :], egf, float(NG - 1), None, ALU.min).then_inc(eg_ready, 1)
                    link(dve.tensor_scalar(kill1, egf, float(NG - 1), FAR, ALU.is_equal, ALU.mult))
                    link(dve.tensor_scalar(koff, egf, float(NG - 1), FAR, ALU.is_gt, ALU.mult))
                    link(dve.scalar_tensor_tensor(out=koff, in0=ntc, scalar=-float(P), in1=koff, op0=ALU.mult, op1=ALU.add))
                    dve.wait_ge(row_mm, 1)
                    for i in range(RB):
                        link(dve.tensor_copy(ntf[0:1, i * RC:(i + 1) * RC], bank[2 + i][0:1, 0:RC]))
                    link(dve.memset(tile_row[0:1, :], 0))
                    link(dve.tensor_copy(tile_row[0:1, PAD:PAD + STEPS], ntf[0:1, 0:STEPS]))
                    if first:
                        link(dve.tensor_tensor(befr[0:1, :], srow[0:1, :], ntf[0:1, :], ALU.subtract))
                        link(dve.tensor_scalar(befr[0:1, :], befr[0:1, :], float(W), float(E - W), ALU.mult, ALU.min))
                        link(dve.tensor_copy(base[:, :], befr[0:1, 0:STEPS]))
                    dve.wait_ge(raw_in, 16 * K * NB)
                    for c in range(NB):
                        step.inc(dve.tensor_scalar(keyf[:, c, 0:DUP], raw[:, 0, c, 0:DUP], koff[:, c:c + 1],
                                                   kill1[:, c:c + 1], ALU.add, ALU.add))
                        link(dve.tensor_scalar(keyf[:, c, DUP:W], raw[:, 0, c, DUP:W], koff[:, c:c + 1], None, ALU.add))
                    if first:
                        link(dve.tensor_copy(srcf, raw[:, 1]))
                        link(dve.tensor_tensor(eqf, raw[:, 0], raw[:, 2], ALU.is_equal))
                        link(dve.tensor_scalar(pen_w, eqf, PEN, -PEN, ALU.mult, ALU.add))
                        link(dve.tensor_tensor(eqf, raw[:, 0], raw[:, 3], ALU.is_equal))
                        dve.tensor_scalar(lastf, eqf, -1.0, 1.0, ALU.mult, ALU.add).then_inc(keys_ready, 1)
                    else:
                        dve.tensor_copy(srcf, raw[:, 1]).then_inc(keys_ready, 1)
                    for c in range(NB):
                        n = min(P, STEPS - c * P)
                        for k, table in enumerate((key, index, flag) if first else (key, index)):
                            q = kinds * c + k
                            dve.wait_ge(turned, q + 1)
                            dve.tensor_copy(table[:, :, c * P:c * P + n],
                                            bank[q % 6][:, 0:W].rearrange("p (g s) -> p g s", g=G)[:, :, 0:n]).then_inc(turned_used, 1)

        step_tables("wide", WIDE, carve(acc), carve(work),
                    eg_col, node_key, src_idx, nt_row, base_row, last_flag, first=True)

        def layer_norm(tag, load_x=False, loads=(), store=False):
            x_in, zeroed = sem(f"x_in{tag}"), sem(f"x_zeroed{tag}")
            ln_dve, ln_std, ln_norm, ln_h = (sem(f"{s}{tag}") for s in ("ln_dve", "ln_std", "ln_norm", "ln_h"))
            h_out, weights_in = sem(f"h_out{tag}"), sem(f"weights_in{tag}")
            with nc.Block() as block:
                @block.sync
                def _(sp):
                    if load_x:
                        sp.dma_start(x_sb[:, 0:NT - 1, :], x[0:(NT - 1) * P, :].rearrange("(t p) f -> p t f", p=P)).then_inc(x_in, 16)
                        sp.wait_ge(zeroed, 1)
                        sp.dma_start(x_sb[0:LAST, NT - 1, :], x[(NT - 1) * P:N, :]).then_inc(x_in, 16)
                    for to, frm in loads:
                        sp.dma_start(to, frm).then_inc(weights_in, 16)
                    if store:
                        sp.wait_ge(ln_h, NT)
                        sp.dma_start(h_rows.rearrange("(t p) f -> p t f", p=P), h_sb[:, :, :]).then_inc(h_out, 16)
                        sp.wait_ge(h_out, 16)
                    if loads:
                        sp.wait_ge(weights_in, 16 * len(loads))

                @block.vector
                def _(dve):
                    step = Count(ln_dve)

                    def link(ins):
                        dve.wait_ge(ln_dve, step.inc(ins))

                    if load_x:
                        dve.memset(x_sb[:, NT - 1, :], 0.0).then_inc(zeroed, 1)
                        dve.wait_ge(x_in, 32)
                    for t in range(NT):
                        step.inc(dve.bn_stats(stats[:, t, :], x_sb[:, t, :]))
                    for t in range(NT):
                        dve.wait_ge(ln_dve, t + 1)
                        step.inc(dve.bn_aggr(mv[:, t, :], stats[:, t, :]))
                    dve.wait_ge(ln_dve, step.n)
                    dve.tensor_scalar(veps[:, :], mv[:, :, 1], EPS, None, ALU.add).then_inc(ln_std, 1)
                    dve.wait_ge(ln_std, 2)
                    link(dve.reciprocal(rstd[:, :], std[:, :]))
                    dve.scalar_tensor_tensor(out=nmr[:, :], in0=mv[:, :, 0], scalar=-1.0, in1=rstd[:, :],
                                             op0=ALU.mult, op1=ALU.mult).then_inc(ln_norm, 1)

                @block.scalar
                def _(act):
                    act.wait_ge(ln_std, 1)
                    act.activation(std[:, :], veps[:, :], ACT.Sqrt).then_inc(ln_std, 1)
                    act.wait_ge(ln_norm, 1)
                    for t in range(NT):
                        act.activation(h_sb[:, t, :], x_sb[:, t, :], ACT.Relu, bias=nmr[:, t:t + 1],
                                       scale=rstd[:, t:t + 1]).then_inc(ln_h, 1)

        w1_sb = work[:, 0:4 * HID].rearrange("p (k n) -> p k n", k=4)
        w2_sb = work[:, 4 * HID:4 * HID + KH * F].rearrange("p (j n) -> p j n", j=KH)
        b1_sb = small[:, 0:KH]
        w1u_sb = small[:, KH:2 * KH]
        u_bc = sv(2 * KH)
        bias1 = small[:, 3 * KH:4 * KH]
        with nc.allow_non_contiguous_dma(reason="bias columns, once"):
            layer_norm("0", load_x=True, loads=[
                (w1_sb, W1[0:4 * P, :].rearrange("(k p) n -> p k n", p=P)),
                (w2_sb, W2.rearrange("(j p) n -> p j n", p=P)),
                (b1_sb, b1.rearrange("(j p) -> p j", p=P)),
                (w1u_sb, W1[4 * P, :].rearrange("(j p) -> p j", p=P)),
                (u_bc, u0[0:1, 0:1].broadcast_to([P, 1])),
                (bias_bc[:, 0, :], b2.rearrange("(a f) -> a f", a=1).broadcast_to([P, F])),
                (bias_bc[:, 1, :], bsage.rearrange("(a f) -> a f", a=1).broadcast_to([P, F])),
            ])

        def run_steps(eng, stages, before=None, plan=WIDE):
            U, IT = plan.U, plan.IT

            def at(t, j, end, loaded):
                for fn, d in stages:
                    tt, jj = t + (j - d) // U, (j - d) % U
                    if isinstance(tt, int) and not 0 <= tt < end:
                        continue
                    fn(tt, jj, loaded[d][j] if loaded is not None and d in loaded else None)

            def iteration(t, end=IT, slots=U):
                loaded = before(t) if before else None
                for j in range(slots):
                    at(t, j, end, loaded)

            iteration(0)
            with eng.Fori(1, IT) as t:
                iteration(t)
            behind = max(d for _, d in stages)
            if behind:
                iteration(IT, IT, behind)

        def tiles_of_steps(t, behind, row=None, U=WIDE.U):
            got = {}
            for d in behind:
                _, got[d] = nc.values_load_multi_w_load_instructions(
                    (nt_row if row is None else row)[0:1, bass.ds(t * U + (PAD - d), U)], engines=DVE_ENGINE, min_val=0, max_val=NT - 1,
                    skip_runtime_bounds_check_because="the table counts tiles")
            return got

        A0 = 2 * F + 1
        acc0 = acc[:, :].rearrange("p (t f) -> p t f", t=NT)
        edges_in = [sem(f"edges_in{j}") for j in range(U)]
        pen_in = [sem(f"pen_in{j}") for j in range(D)]
        cleared, one_hot, one_hot_last = sem("cleared"), sem("one_hot"), sem("one_hot_last")
        edges_turned, scanned, max_turned, max_copied = sem("edges_turned"), sem("scanned"), sem("max_turned"), sem("max_copied")
        edges_used, sums_ready, sums_added, bias_made = sem("edges_used"), sem("sums_ready"), sem("sums_added"), sem("bias_made")
        xT = [bank[0][:, 0:W], bank[1][:, 0:W]]
        sT = [bank[2][:, 0:W], bank[3][:, 0:W]]
        sums = [bank[4 + j % D] for j in range(U)]
        onehot_last = carve(work[:, 4 * HID + KH * F:WORK])(D, G, P)

        with nc.Block() as block:
            @block.sync
            def _(sp):
                def load(t, j, _):
                    s = t * U + j
                    sp.wait_ge(edges_used, s + 1)
                    sp.dma_start(edge_buf[:, j, :, 0:F],
                                 edge_attr[bass.ds(bases[j], W), :].rearrange("(g p) f -> p g f", p=P)).then_inc(edges_in[j], 16)
                    sp.wait_ge(scanned, s + 1)
                    sp.dma_start(pen_buf[:, j % D, :], pen_rows[bass.ds(s, 1), :].broadcast_to([P, W])).then_inc(pen_in[j % D], 16)

                with sp.Fori(0, IT) as t:
                    _, bases = nc.values_load_multi_w_load_instructions(
                        base_row[0:1, bass.ds(t * U, U)], engines=SP_ENGINE, min_val=0, max_val=E - W,
                        skip_runtime_bounds_check_because="the table is cut at E - W")
                    for j in range(U):
                        load(t, j, None)

            @block.gpsimd
            def _(pool):
                pool.memset(edge_buf[:, :, :, F:F + 1], 1.0).then_inc(cleared, 1)
                pool.memset(acc[:, :], 0.0).then_inc(cleared, 1)

            @block.tensor
            def _(pe):
                pe.sem_inc(edges_used, U)
                pe.sem_inc(sums_ready, D)
                pe.sem_inc(max_turned, 2)
                pe.wait_ge(cleared, 2)

                def turn(t, j, _):
                    s = t * U + j
                    pe.wait_ge(edges_in[j], 16 * (t + 1))
                    pe.wait_ge(scanned, s + D - 1)
                    for g in range(G):
                        last = pe.transpose(xT[j % 2][:, g * P:(g + 1) * P], edge_buf[:, j, g, 0:F], ident[:, :])
                    last.then_inc(edges_turned, 1)

                def total(t, j, _):
                    s = t * U + j
                    pe.wait_ge(one_hot, s + 1)
                    pe.wait_ge(sums_added, s + 1)
                    for g in range(G):
                        last = pe.matmul(sums[j][:, 0:F + 1], onehot[:, j % D, g, :], edge_buf[:, j, g, 0:F + 1],
                                         start=(g == 0), stop=(g == G - 1))
                    last.then_inc(edges_used, 1)

                def turn_back(t, j, _):
                    s = t * U + j
                    pe.wait_ge(scanned, s + D + 1)
                    pe.wait_ge(max_copied, s + 1)
                    for g in range(G):
                        last = pe.transpose(sT[j % 2][:, g * P:(g + 1) * P], scan_buf[:, j % 2, g * P:(g + 1) * P], ident[:, :])
                    last.then_inc(max_turned, 1)

                def maxima(t, j, _):
                    s = t * U + j
                    pe.wait_ge(max_copied, s + 3)
                    pe.wait_ge(one_hot_last, s + D + 1)
                    for g in range(G):
                        last = pe.matmul(sums[j][:, F + 1:A0], onehot_last[:, j % D, g, :], lastmax[:, j % 2, g, :],
                                         start=(g == 0), stop=(g == G - 1))
                    last.then_inc(sums_ready, 1)

                run_steps(pe, [(turn, 0), (total, 1), (turn_back, 2), (maxima, 3)])

            @block.scalar
            def _(act):
                act.sem_inc(max_copied, 2)
                act.activation(bias1, w1u_sb, ACT.Copy, scale=u_bc).then_inc(bias_made, 1)
                act.sem_inc(one_hot_last, D)

                def last_hots(t, j, _):
                    s = t * U + j
                    act.wait_ge(one_hot, s + 1)
                    act.wait_ge(sums_ready, s + 1)
                    for g in range(G):
                        last = act.activation(onehot_last[:, j % D, g, :], onehot[:, j % D, g, :], ACT.Copy,
                                              scale=last_flag[:, g, bass.ds(s, 1)])
                    last.then_inc(one_hot_last, 1)

                def copy_maxima(t, j, _):
                    s = t * U + j
                    act.wait_ge(max_turned, s + 3)
                    act.wait_ge(sums_ready, s + D - 1)
                    act.activation(lastmax[:, j % 2, :, :], sT[j % 2].rearrange("p (g f) -> p g f", g=G), ACT.Copy).then_inc(max_copied, 1)

                run_steps(act, [(last_hots, 0), (copy_maxima, 2)])

            @block.vector
            def _(dve):
                dve.sem_inc(scanned, D)
                dve.sem_inc(sums_added, D)
                dve.wait_ge(bias_made, 1)
                dve.tensor_tensor(bias1, bias1, b1_sb, ALU.add).then_inc(bias_made, 1)
                dve.memset(scan_buf[:, 1, W - 1:W], 0.0).then_inc(bias_made, 1)
                dve.wait_ge(bias_made, 3)
                dve.wait_ge(cleared, 2)

                def one_hots(t, j, _):
                    s = t * U + j
                    dve.wait_ge(edges_used, s + 1 + U - D)
                    dve.wait_ge(one_hot_last, s + 1)
                    dve.tensor_tensor(onehot[:, j % D, :, :], iota_n[:, :].rearrange("p (a n) -> p a n", a=1).broadcast_to([P, G, P]),
                                      node_key[:, :, bass.ds(s, 1)].broadcast_to([P, G, P]), ALU.is_equal).then_inc(one_hot, 1)

                def scan(t, j, _):
                    s = t * U + j
                    dve.wait_ge(edges_turned, s + 1)
                    dve.wait_ge(pen_in[j % D], 16 * (t + 1))
                    dve.wait_ge(scanned, s + D)
                    dve.wait_ge(max_turned, s + 1)
                    dve.tensor_tensor_scan(scan_buf[:, j % 2, :], pen_buf[:, j % D, :], xT[j % 2],
                                           scan_buf[:, (j - 1) % 2, W - 1:W], ALU.add, ALU.max).then_inc(scanned, 1)

                def add(t, j, tile):
                    s = t * U + j
                    dve.wait_ge(sums_ready, s + D + 1)
                    dve.wait_ge(sums_added, s + D)
                    row = acc0[:, bass.ds(tile, 1), :].rearrange("p a f -> p (a f)")
                    dve.tensor_tensor(row, row, sums[j][:, 0:A0], ALU.add).then_inc(sums_added, 1)

                run_steps(dve, [(one_hots, 0), (scan, 1), (add, 4)], before=lambda t: tiles_of_steps(t, [4]))

        turned_sb = work[:, 4 * HID + KH * F:4 * HID + KH * F + 4 * CW].rearrange("p (k n) -> p k n", k=4)
        gelu_sb = work[:, 4 * HID + KH * F + 4 * CW:WORK].rearrange("p (j n) -> p j n", j=KH)

        def chunks(eng, body):
            with eng.Fori(0, NC) as c:
                body(c, CT)
            for c in range(NC, NC + NT - NC * CT):
                body(NC, NT - NC * CT)

        def tiles(c, n):
            return bass.ds(c * CT, n)

        class Dense:

            def __init__(self, tag, K):
                self.K = K
                self.staged, self.copied_in, self.turned, self.copied, self.out, self.added = (
                    sem(f"{tag}_{s}") for s in ("staged", "copied_in", "turned", "copied", "out", "added"))

        d0 = Dense("mlp", 4)
        hid_ready, hid_done, acc_rd = sem("hid_ready"), sem("hid_done"), sem("rdeg_made")
        b2_bc = bias_bc[:, 0, :].rearrange("p (a f) -> p a f", a=1)
        bs_bc = bias_bc[:, 1, :].rearrange("p (a f) -> p a f", a=1)
        with nc.Block() as block:
            @block.gpsimd
            def _(pool):
                def copy_in(c, n):
                    pool.wait_ge(d0.turned, 4 * c + 4)
                    pool.tensor_copy(stage[:, 0:n, 0, :], h_sb[:, tiles(c, n), :]).then_inc(d0.copied_in, 1)
                    pool.tensor_copy(stage[:, 0:n, 1, :], acc0[:, tiles(c, n), 0:F]).then_inc(d0.copied_in, 1)
                    pool.tensor_copy(stage[:, 0:n, 2, :], acc0[:, tiles(c, n), F + 1:A0]).then_inc(d0.copied_in, 1)

                chunks(pool, copy_in)

            @block.tensor
            def _(pe):
                pe.sem_inc(d0.turned, 4)
                pe.sem_inc(d0.out, 1)

                def chunk(c, n):
                    pe.wait_ge(d0.staged, c + 1)
                    pe.wait_ge(d0.copied_in, 3 * c + 3)
                    for k in range(4):
                        for i in range(n):
                            last = pe.transpose(bank[k][:, i * P:(i + 1) * P], stage[:, i, k, :], ident[:, :])
                        last.then_inc(d0.turned, 1)
                    pe.wait_ge(d0.copied, 4 * c + 4)
                    for j in range(KH):
                        pe.wait_ge(hid_done, KH * c + j + 1)
                        for k in range(4):
                            last = pe.matmul(bank[4 + j % 2][:, 0:n * P], w1_sb[:, k, j * P:(j + 1) * P],
                                             turned_sb[:, k, 0:n * P], start=(k == 0), stop=(k == 3))
                        last.then_inc(hid_ready, 1)
                    pe.wait_ge(hid_done, KH * c + KH + 2)
                    pe.wait_ge(d0.added, c + 1)
                    for i in range(n):
                        for j in range(KH):
                            last = pe.matmul(bank[6][:, i * F:(i + 1) * F], gelu_sb[:, j, i * P:(i + 1) * P],
                                             w2_sb[:, j, :], start=(j == 0), stop=(j == KH - 1))
                    last.then_inc(d0.out, 1)

                chunks(pe, chunk)

            @block.scalar
            def _(act):
                act.sem_inc(hid_done, 2)

                def chunk(c, n):
                    for k in range(4):
                        act.wait_ge(d0.turned, 4 * c + 4 + k + 1)
                        act.activation(turned_sb[:, k, 0:n * P], bank[k][:, 0:n * P], ACT.Copy).then_inc(d0.copied, 1)
                    act.wait_ge(d0.out, c + 1)
                    for j in range(KH):
                        act.wait_ge(hid_ready, KH * c + j + 1)
                        act.activation(gelu_sb[:, j, 0:n * P], bank[4 + j % 2][:, 0:n * P], ACT.Gelu,
                                       bias=bias1[:, j:j + 1]).then_inc(hid_done, 1)

                chunks(act, chunk)

            @block.vector
            def _(dve):
                dve.sem_inc(d0.added, 1)
                dve.tensor_scalar(deg[:, :], acc0[:, :, F], 1.0, None, ALU.max).then_inc(acc_rd, 1)
                dve.wait_ge(acc_rd, 1)
                dve.reciprocal(rdeg[:, :], deg[:, :]).then_inc(acc_rd, 1)
                dve.wait_ge(acc_rd, 2)

                def mean(c, n):
                    dve.wait_ge(d0.turned, 4 * c + 4)
                    dve.tensor_tensor(stage[:, 0:n, 3, :], acc0[:, tiles(c, n), 0:F],
                                      rdeg[:, tiles(c, n)].rearrange("p (t a) -> p t a", a=1).broadcast_to([P, n, F]),
                                      ALU.mult).then_inc(d0.staged, 1)

                def residual(c, n):
                    xs = x_sb[:, tiles(c, n), :]
                    dve.tensor_tensor(xs, xs, h_sb[:, tiles(c, n), :], ALU.add).then_inc(acc_rd, 1)
                    dve.wait_ge(acc_rd, 2 * c + 3)
                    dve.tensor_tensor(xs, xs, b2_bc.broadcast_to([P, n, F]), ALU.add).then_inc(acc_rd, 1)
                    dve.wait_ge(acc_rd, 2 * c + 4)
                    dve.wait_ge(d0.out, c + 2)
                    dve.tensor_tensor(xs, xs, bank[6][:, 0:n * F].rearrange("p (t f) -> p t f", f=F), ALU.add).then_inc(d0.added, 1)

                def both(c, n):
                    mean(c, n)
                    residual(c, n)

                chunks(dve, both)

        recycle_semaphores()
        layer_norm("1", store=True, loads=[(a_bc[:, :], agat.rearrange("h a b -> (b h a)").rearrange("(b n) -> b n", b=1).broadcast_to([P, HEADS * (2 * HO + EA)]))])

        step_tables("fine", FINE, carve(acc), carve(step_mem), eg_fine, key_fine, src_idx_fine, nt_row_fine)

        acc1 = acc[:, 0:NT * F].rearrange("p (t f) -> p t f", t=NT)

        def gather(pool, plan, rows, to, got, index_ready, go):
            with pool.Fori(0, plan.IT) as t:
                for j in range(plan.U):
                    pool.wait_ge(index_ready, t * plan.U + j + 1)
                    pool.sem_inc(go, 1)
                    for g in range(plan.G):
                        i = j * plan.G + g
                        pool.indirect_dma_start(to[:, j, g, :], None, rows[:, :],
                                                bass.IndirectOffsetOnAxis(ap=idx_now[:, i:i + 1], axis=0)).then_inc(got[j], 16)

        def place_indices(act, plan, table, t, j, slots_free, index_ready, go):
            s = t * plan.U + j
            act.wait_ge(slots_free, s + 1)
            act.sem_inc(go, 1)
            act.activation(idx_now[:, j * plan.G:(j + 1) * plan.G], table[:, :, bass.ds(s, 1)].rearrange("p g a -> p (g a)"), ACT.Copy).then_inc(index_ready, 1)

        take = carve(step_mem)
        rows_fine = take(FINE.U, FINE.G, F)
        onehot_fine = take(FINE.D, FINE.G, P)

        def sum_sources(tag):
            G, U, D = FINE.G, FINE.U, FINE.D
            got = [sem(f"{tag}_rows_in{j}") for j in range(U)]
            placed, go, act_go, hot, used, added, clear = (sem(f"{tag}_{s}") for s in (
                "indices_placed", "go", "act_go", "one_hot", "rows_used", "added", "cleared"))
            with nc.Block() as block:
                @block.gpsimd
                def _(pool):
                    gather(pool, FINE, h_rows, rows_fine, got, placed, go)

                @block.scalar
                def _(act):
                    with act.Fori(0, FINE.IT) as t:
                        for j in range(U):
                            place_indices(act, FINE, src_idx_fine, t, j, used, placed, act_go)

                @block.tensor
                def _(pe):
                    pe.sem_inc(used, U)

                    def total(t, j, _):
                        s = t * U + j
                        pe.wait_ge(got[j], 16 * G * (t + 1))
                        pe.wait_ge(hot, s + 1)
                        pe.wait_ge(added, s + 1)
                        for g in range(G):
                            last = pe.matmul(bank[j % D][:, 0:F], onehot_fine[:, j % D, g, :], rows_fine[:, j, g, :],
                                             start=(g == 0), stop=(g == G - 1))
                        last.then_inc(used, 1)

                    run_steps(pe, [(total, 0)], plan=FINE)

                @block.vector
                def _(dve):
                    dve.sem_inc(added, D)
                    dve.memset(acc[:, 0:NT * F], 0.0).then_inc(clear, 1)
                    dve.wait_ge(clear, 1)

                    def hots(t, j, _):
                        s = t * U + j
                        dve.wait_ge(used, s + 1 + U - D)
                        for g in range(G):
                            last = dve.tensor_scalar(onehot_fine[:, j % D, g, :], iota_n[:, :], key_fine[:, g, bass.ds(s, 1)], None, ALU.is_equal)
                        last.then_inc(hot, 1)

                    def add(t, j, tile):
                        s = t * U + j
                        dve.wait_ge(used, s + U + 1)
                        dve.wait_ge(added, s + D)
                        row = acc1[:, bass.ds(tile, 1), :].rearrange("p a f -> p (a f)")
                        dve.tensor_tensor(row, row, bank[j % D][:, 0:F], ALU.add).then_inc(added, 1)

                    run_steps(dve, [(hots, 0), (add, 2)], before=lambda t: tiles_of_steps(t, [2], nt_row_fine, FINE.U), plan=FINE)


        def stage_means(dve, d, c, n):
            dve.wait_ge(d.turned, 2 * c + 2)
            dve.tensor_tensor(stage[:, 0:n, 0, :], acc1[:, tiles(c, n), :],
                              rdeg[:, tiles(c, n)].rearrange("p (t a) -> p t a", a=1).broadcast_to([P, n, F]),
                              ALU.mult).then_inc(d.staged, 1)

        def stage_own(pool, d, c, n):
            pool.wait_ge(d.turned, 2 * c + 2)
            pool.tensor_copy(stage[:, 0:n, 1, :], h_sb[:, tiles(c, n), :]).then_inc(d.copied_in, 1)

        def turn_two(pe, d, c, n):
            pe.wait_ge(d.staged, c + 1)
            pe.wait_ge(d.copied_in, c + 1)
            pe.wait_ge(d.copied, 2 * c + 2)
            for k in range(2):
                for i in range(n):
                    last = pe.transpose(bank[k][:, i * P:(i + 1) * P], stage[:, i, k, :], ident[:, :])
                last.then_inc(d.turned, 1)
            pe.wait_ge(d.copied, 2 * c + 4)
            pe.wait_ge(d.added, c + 1)

        def copy_two(act, d, c, n):
            act.wait_ge(d.out, c + 1)
            for k in range(2):
                act.wait_ge(d.turned, 2 * c + 2 + k + 1)
                act.activation(turn2[:, k, 0:n * P], bank[k][:, 0:n * P], ACT.Copy).then_inc(d.copied, 1)

        sum_sources("l1")

        out_t = acc[:, NT * F:NT * F + NT * P]
        d1 = Dense("l1d", 2)
        w_in, n_sum, n_chain, n_sq, n_std, n_ready = (sem(f"l1_{s}") for s in ("weights_in", "sum", "chain", "squares", "std", "norm_ready"))
        g_done, g_turned, g_added = sem("l1_gelu"), sem("l1_gelu_turned"), sem("l1_gelu_added")
        bl_c, gw_c, gb_c, gms_c, tot, mean_c, shift, ssq, var_c, std_c, scale_c, beta_c = (sv(32 + i) for i in range(12))
        with nc.Block() as block:
            @block.sync
            def _(sp):
                sp.dma_start(wt[:, 0, :], Wl).then_inc(w_in, 16)
                sp.dma_start(wt[:, 1, :], Wr).then_inc(w_in, 16)
                with nc.allow_non_contiguous_dma(reason="bias columns, once"):
                    for to, frm in ((bl_c, bl), (gw_c, gw), (gb_c, gb), (gms_c, gms)):
                        sp.dma_start(to, frm.rearrange("(p a) -> p a", a=1)).then_inc(w_in, 16)

            @block.gpsimd
            def _(pool):
                chunks(pool, lambda c, n: stage_own(pool, d1, c, n))

            @block.tensor
            def _(pe):
                pe.sem_inc(d1.turned, 2)
                pe.sem_inc(d1.out, 1)
                pe.wait_ge(w_in, 96)

                def chunk(c, n):
                    turn_two(pe, d1, c, n)
                    for k in range(2):
                        last = pe.matmul(bank[2][:, 0:n * P], wt[:, k, :], turn2[:, k, 0:n * P], start=(k == 0), stop=(k == 1))
                    last.then_inc(d1.out, 1)

                chunks(pe, chunk)
                pe.sem_inc(g_turned, 1)

                def back(c, n):
                    pe.wait_ge(g_done, c + 1)
                    pe.wait_ge(g_added, c + 1)
                    for i in range(n):
                        last = pe.transpose(bank[3][:, i * F:(i + 1) * F], gelu_t[:, i * P:(i + 1) * P], ident[:, :])
                    last.then_inc(g_turned, 1)

                chunks(pe, back)

            @block.scalar
            def _(act):
                act.sem_inc(d1.copied, 2)
                act.sem_inc(d1.added, 1)
                act.wait_ge(w_in, 96)

                def chunk(c, n):
                    copy_two(act, d1, c, n)
                    act.wait_ge(d1.out, c + 2)
                    act.activation(out_t[:, bass.ds(c * CW, n * P)], bank[2][:, 0:n * P], ACT.Identity,
                                   bias=bl_c).then_inc(d1.added, 1)

                chunks(act, chunk)
                act.wait_ge(n_sum, 1)
                act.activation(acc[:, 0:N], out_t[:, 0:N], ACT.Square, bias=shift, accum_out=ssq).then_inc(n_sq, 1)
                act.wait_ge(n_std, 1)
                act.activation(std_c, var_c, ACT.Sqrt).then_inc(n_std, 1)
                act.wait_ge(n_ready, 1)

                def gelu(c, n):
                    act.wait_ge(g_turned, c + 1)
                    act.activation(gelu_t[:, 0:n * P], out_t[:, bass.ds(c * CW, n * P)], ACT.Gelu,
                                   bias=beta_c, scale=scale_c).then_inc(g_done, 1)

                chunks(act, gelu)

            @block.vector
            def _(dve):
                step = Count(n_chain)

                def link(ins):
                    dve.wait_ge(n_chain, step.inc(ins))

                chunks(dve, lambda c, n: stage_means(dve, d1, c, n))
                dve.wait_ge(d1.added, NC + 1 + NT - NC * CT)
                link(dve.tensor_reduce(tot, out_t[:, 0:N], AX.X, ALU.add))
                link(dve.tensor_scalar(mean_c, tot, 1.0 / N, None, ALU.mult))
                dve.scalar_tensor_tensor(out=shift, in0=mean_c, scalar=-1.0, in1=gms_c, op0=ALU.mult, op1=ALU.mult).then_inc(n_sum, 1)
                dve.wait_ge(n_sq, 1)
                dve.tensor_scalar(var_c, ssq, 1.0 / N, EPS, ALU.mult, ALU.add).then_inc(n_std, 1)
                dve.wait_ge(n_std, 2)
                link(dve.reciprocal(std_c, std_c))
                link(dve.tensor_tensor(scale_c, gw_c, std_c, ALU.mult))
                link(dve.tensor_tensor(beta_c, scale_c, shift, ALU.mult))
                dve.tensor_tensor(beta_c, beta_c, gb_c, ALU.add).then_inc(n_ready, 1)
                base = step.n

                def residual(c, n):
                    xs = x_sb[:, tiles(c, n), :]
                    dve.tensor_tensor(xs, xs, h_sb[:, tiles(c, n), :], ALU.add).then_inc(n_chain, 1)
                    dve.wait_ge(n_chain, base + 1 + c)
                    dve.wait_ge(g_turned, c + 2)
                    dve.tensor_tensor(xs, xs, bank[3][:, 0:n * F].rearrange("p (t f) -> p t f", f=F), ALU.add).then_inc(g_added, 1)

                dve.sem_inc(g_added, 1)
                chunks(dve, residual)

        layer_norm("2", store=True)
        sum_sources("l2")

        d2 = Dense("l2d", 2)
        w2_in, w2_turned, w2_copied, x_chain = sem("l2_weights_in"), sem("l2_weights_turned"), sem("l2_weights_copied"), sem("l2_chain")
        w_raw = gelu_t[:, 0:2 * F]
        with nc.Block() as block:
            @block.sync
            def _(sp):
                sp.dma_start(w_raw, Wsage).then_inc(w2_in, 16)

            @block.gpsimd
            def _(pool):
                chunks(pool, lambda c, n: stage_own(pool, d2, c, n))

            @block.tensor
            def _(pe):
                pe.sem_inc(d2.turned, 2)
                pe.sem_inc(d2.out, 1)
                pe.wait_ge(w2_in, 16)
                for k in range(2):
                    last = pe.transpose(bank[3][:, k * F:(k + 1) * F], w_raw[:, k * F:(k + 1) * F], ident[:, :])
                last.then_inc(w2_turned, 1)
                pe.wait_ge(w2_copied, 1)

                def chunk(c, n):
                    turn_two(pe, d2, c, n)
                    for i in range(n):
                        for k in range(2):
                            last = pe.matmul(bank[2][:, i * F:(i + 1) * F], turn2[:, k, i * P:(i + 1) * P], wt[:, 1 - k, :],
                                             start=(k == 0), stop=(k == 1))
                    last.then_inc(d2.out, 1)

                chunks(pe, chunk)

            @block.scalar
            def _(act):
                act.sem_inc(d2.copied, 2)
                act.wait_ge(w2_turned, 1)
                act.activation(wt[:, 0:2, :].rearrange("p k n -> p (k n)"), bank[3][:, 0:2 * F], ACT.Copy).then_inc(w2_copied, 1)
                chunks(act, lambda c, n: copy_two(act, d2, c, n))

            @block.vector
            def _(dve):
                dve.sem_inc(d2.added, 1)

                def chunk(c, n):
                    stage_means(dve, d2, c, n)
                    xs = x_sb[:, tiles(c, n), :]
                    dve.tensor_tensor(xs, xs, bs_bc.broadcast_to([P, n, F]), ALU.add).then_inc(x_chain, 1)
                    dve.wait_ge(x_chain, c + 1)
                    dve.wait_ge(d2.out, c + 2)
                    dve.tensor_tensor(xs, xs, bank[2][:, 0:n * F].rearrange("p (t f) -> p t f", f=F), ALU.add).then_inc(d2.added, 1)

                chunks(dve, chunk)

        recycle_semaphores()
        layer_norm("3")

        av = a_bc[:, :].rearrange("p (h a) -> p h a", h=HEADS)
        take = carve(acc)
        raw8 = take(2, W, EA)
        srow8 = take(2, HEADS, W)
        ea_in = [sem("ea_in0"), sem("ea_in1")]
        mac, scores_turned, scores_copied = sem("score_products"), sem("scores_turned"), sem("scores_copied")
        MC = HEADS * EA
        with nc.Block() as block:
            @block.gpsimd
            def _(pool):
                for c in range(NB):
                    if c >= 2:
                        pool.wait_ge(mac, MC * (c - 1))
                    pool.indirect_dma_start(raw8[:, c % 2].rearrange("p e k -> p (e k)"), None, ea8_rows[:, :],
                                            bass.IndirectOffsetOnAxis(ap=eg_col[:, c:c + 1], axis=0)).then_inc(ea_in[c % 2], 16)

            @block.vector
            def _(dve):
                n = 0
                for c in range(NB):
                    dve.wait_ge(ea_in[c % 2], 16 * (c // 2 + 1))
                    if c >= 2:
                        dve.wait_ge(scores_turned, HEADS * (c - 1))
                    for k in range(EA):
                        for h in range(HEADS):
                            a = av[:, h, 2 * HO + k:2 * HO + k + 1]
                            o = srow8[:, c % 2, h, :]
                            if k:
                                dve.wait_ge(mac, n + 1 - HEADS)
                                ins = dve.scalar_tensor_tensor(out=o, in0=raw8[:, c % 2, :, k], scalar=a, in1=o,
                                                               op0=ALU.mult, op1=ALU.add)
                            else:
                                ins = dve.tensor_scalar(o, raw8[:, c % 2, :, k], a, None, ALU.mult)
                            ins.then_inc(mac, 1)
                            n += 1

            @block.tensor
            def _(pe):
                for c in range(NB):
                    pe.wait_ge(mac, MC * (c + 1))
                    for h in range(HEADS):
                        q = c * HEADS + h
                        if q >= 8:
                            pe.wait_ge(scores_copied, q - 7)
                        for g in range(G):
                            last = pe.transpose(bank[q % 8][:, g * P:(g + 1) * P], srow8[:, c % 2, h, g * P:(g + 1) * P], ident[:, :])
                        last.then_inc(scores_turned, 1)

            @block.scalar
            def _(act):
                for c in range(NB):
                    n = min(P, STEPS - c * P)
                    for h in range(HEADS):
                        q = c * HEADS + h
                        act.wait_ge(scores_turned, q + 1)
                        act.activation(score_e[:, h, :, c * P:c * P + n],
                                       bank[q % 8][:, 0:W].rearrange("p (g s) -> p g s", g=G)[:, :, 0:n], ACT.Copy).then_inc(scores_copied, 1)

        xrow = acc[:, 0:NT * RW].rearrange("p (t h w) -> p t h w", t=NT, h=HEADS)
        node_tab = sb("node_tab", [P, NT, 3 * HEADS])
        d3 = Dense("l3d", 1)
        w3_in, t_chain, t_out, ones_set = sem("l3_weights_in"), sem("l3_chain"), sem("l3_table_out"), sem("l3_ones")
        prod = gelu_t
        as_bc = av[:, :, 0:HO].rearrange("p h (a o) -> p a h o", a=1)
        ad_bc = av[:, :, HO:2 * HO].rearrange("p h (a o) -> p a h o", a=1)
        with nc.Block() as block:
            @block.sync
            def _(sp):
                sp.dma_start(wt[:, 0, :].rearrange("p (h o) -> p h o", h=HEADS), Wgat.rearrange("h i o -> i h o")).then_inc(w3_in, 16)
                sp.wait_ge(t_chain, 5 * (NC + NT - NC * CT))
                sp.wait_ge(ones_set, 1)
                sp.dma_start(xt_rows.rearrange("(t p) w -> p t w", p=P), xrow.rearrange("p t h w -> p t (h w)")).then_inc(t_out, 16)
                sp.wait_ge(t_out, 16)

            @block.gpsimd
            def _(pool):
                pool.memset(xrow[:, :, :, HO:HO + 1].rearrange("p t h w -> p (t h) w"), 1.0).then_inc(ones_set, 1)

                def copy_in(c, n):
                    pool.wait_ge(d3.turned, c + 1)
                    pool.tensor_copy(stage[:, 0:n, 0, :], h_sb[:, tiles(c, n), :]).then_inc(d3.copied_in, 1)

                chunks(pool, copy_in)

            @block.tensor
            def _(pe):
                pe.sem_inc(d3.turned, 1)
                pe.sem_inc(d3.out, 1)
                pe.wait_ge(w3_in, 16)

                def chunk(c, n):
                    pe.wait_ge(d3.copied_in, c + 1)
                    pe.wait_ge(d3.copied, c + 1)
                    for i in range(n):
                        last = pe.transpose(bank[0][:, i * P:(i + 1) * P], stage[:, i, 0, :], ident[:, :])
                    last.then_inc(d3.turned, 1)
                    pe.wait_ge(d3.copied, c + 2)
                    pe.wait_ge(t_chain, 5 * c + 1)
                    for i in range(n):
                        last = pe.matmul(bank[2][:, i * F:(i + 1) * F], turn2[:, 0, i * P:(i + 1) * P], wt[:, 0, :], start=True, stop=True)
                    last.then_inc(d3.out, 1)

                chunks(pe, chunk)

            @block.scalar
            def _(act):
                act.sem_inc(d3.copied, 1)

                def chunk(c, n):
                    act.wait_ge(d3.out, c + 1)
                    act.wait_ge(d3.turned, c + 2)
                    act.activation(turn2[:, 0, 0:n * P], bank[0][:, 0:n * P], ACT.Copy).then_inc(d3.copied, 1)

                chunks(act, chunk)

            @block.vector
            def _(dve):
                dve.memset(node_tab[:, :, HEADS:3 * HEADS], -BIG).then_inc(t_chain, 1)

                def chunk(c, n):
                    y = bank[2][:, 0:n * F].rearrange("p (t h o) -> p t h o", h=HEADS, o=HO)
                    pr = prod[:, 0:n * F].rearrange("p (t h o) -> p t h o", h=HEADS, o=HO)
                    dve.wait_ge(d3.out, c + 2)
                    dve.wait_ge(t_chain, 5 * c + 1)
                    dve.tensor_scalar(xrow[:, tiles(c, n), :, 0:HO], y, 1.0, None, ALU.mult).then_inc(t_chain, 1)
                    dve.tensor_tensor(pr, y, as_bc.broadcast_to([P, n, HEADS, HO]), ALU.mult).then_inc(t_chain, 1)
                    dve.wait_ge(t_chain, 5 * c + 3)
                    dve.tensor_reduce(xrow[:, tiles(c, n), :, HO + 1], pr, AX.X, ALU.add).then_inc(t_chain, 1)
                    dve.wait_ge(t_chain, 5 * c + 4)
                    dve.tensor_tensor(pr, y, ad_bc.broadcast_to([P, n, HEADS, HO]), ALU.mult).then_inc(t_chain, 1)
                    dve.wait_ge(t_chain, 5 * c + 5)
                    dve.tensor_reduce(node_tab[:, tiles(c, n), 0:HEADS], pr, AX.X, ALU.add).then_inc(t_chain, 1)

                chunks(dve, chunk)

        acc3 = acc[:, 0:NT * HEADS * HW].rearrange("p (t h w) -> p t h w", t=NT, h=HEADS)
        U, IT = DEEP.U, DEEP.IT
        GH = G * HEADS
        take = carve(h_sb[:, :, :].rearrange("p t f -> p (t f)"))
        onehot = take(U, G, P)
        onehot_last = take(4, G, P)
        take = carve(acc[:, NT * HEADS * HW:])
        onehot_t = take(4, G, P)
        weighted = take(2, GH, HW)
        scan_buf = take(2, W)
        take = carve(step_mem)
        edge_buf = take(U, G, RW)
        rows3 = edge_buf.rearrange("p u g (h w) -> p u (g h) w", w=HW + 1)
        pen_buf = take(D, W // 2).bitcast(BF16)
        src_score, max_one = take(D, GH), take(D, G, HEADS + 1)
        node_now = take(D, 3 * HEADS)
        absent, m_sum, m_drop, alpha = take(D, 1), take(D, HEADS), take(D, HEADS), take(D, HEADS)
        e_sum, e_relu, e_diff, weight = (take(D, GH) for _ in range(4))
        ones_row = take(STEPS)
        TARGET, TOP, SRC_TOP = (slice(k * HEADS, (k + 1) * HEADS) for k in range(3))
        hotT = bank[0][:, 0:W]
        scoreT = bank[1][0:HEADS, 0:W]
        maxT = bank[2][:, 0:GH]
        nodeM = [bank[3 + q][:, 0:HEADS + 1] for q in range(2)]
        edgeV = bank[5][:, 0:G * 2 * HEADS].rearrange("p (g k) -> p g k", g=G)
        total = [bank[6][:, 0:HEADS * HW], bank[7][:, 0:HEADS * HW]]
        got3 = [sem(f"l3_rows_in{j}") for j in range(U)]
        pen3_in = [sem(f"l3_pen_in{j}") for j in range(D)]
        (idx3, rows_used, scored, hot3, score_turned, hot_turned, hot_copied, last_made, scan3, max_back, max_in, node_max,
         absent_made, target_in, src_top, sum_made, top_made, dropped, table_kept, alpha_made,
         edge_values, e_sum_made, e_relu_made, e_ready, weights_made, total_ready, rescaled, added, flags, last_set) = (
             sem(f"l3_{s}") for s in (
                 "indices", "rows_used", "scored", "one_hot", "scores_turned", "one_hot_turned", "one_hot_copied", "last_made",
                 "scanned", "maxima_back", "maxima_in", "node_max", "absent", "target_in", "src_top", "top_sum", "top",
                 "dropped", "table_kept", "alpha", "edge_values", "e_sum", "e_relu", "e_ready", "weights", "total",
                 "rescaled", "added", "flags", "last_set"))
        rows_free, scan_seen, slot_free = sem("l3_rows_free"), sem("l3_scan_seen"), sem("l3_slot_free")
        with nc.Block() as block:
            @block.sync
            def _(sp):
                sp.wait_ge(flags, 1)
                sp.dma_start(last_flag[P - 1:P, G - 1, :], ones_row[0:1, :]).then_inc(last_set, 16)
                with sp.Fori(0, IT) as t:
                    for j in range(U):
                        s = t * U + j
                        sp.wait_ge(scan3, s + 1)
                        sp.dma_start(pen_buf[0:HEADS, j % D, :],
                                     pen_rows[bass.ds(s, 1), :].broadcast_to([HEADS, W])).then_inc(pen3_in[j % D], 16)

            @block.gpsimd
            def _(pool):
                gather(pool, DEEP, xt_rows, edge_buf, got3, idx3, rows_free)

            @block.tensor
            def _(pe):
                def turn_hots(t, j, _):
                    s = t * U + j
                    pe.wait_ge(hot3, s + 1)
                    pe.wait_ge(hot_copied, s + 1)
                    for g in range(G):
                        last = pe.transpose(hotT[:, g * P:(g + 1) * P], onehot[:, j, g, :], ident[:, :])
                    last.then_inc(hot_turned, 1)

                def turn_scores(t, j, _):
                    s = t * U + j
                    pe.wait_ge(scored, s + 1)
                    pe.wait_ge(scan3, s + D)
                    for g in range(G):
                        last = pe.transpose(scoreT[:, g * P:(g + 1) * P], src_score[:, j % D, g * HEADS:(g + 1) * HEADS], ident[:, :])
                    last.then_inc(score_turned, 1)

                def turn_back(t, j, _):
                    s = t * U + j
                    pe.wait_ge(scan3, s + D + 1)
                    pe.sem_inc(scan_seen, 1)
                    for g in range(G):
                        last = pe.transpose(maxT[:, g * HEADS:(g + 1) * HEADS], scan_buf[0:HEADS, j % 2, g * P:(g + 1) * P],
                                            ident[0:HEADS, 0:HEADS])
                    last.then_inc(max_back, 1)

                def to_edges(t, j, _):
                    s = t * U + j
                    pe.wait_ge(top_made, s + 1)
                    pe.wait_ge(e_ready, s + 1)
                    for g in range(G):
                        last = pe.matmul(edgeV[:, g, :], onehot_t[:, j % 4, g, :], node_now[:, j % D, 0:2 * HEADS], start=True, stop=True)
                    last.then_inc(edge_values, 1)

                def maxima(t, j, _):
                    s = t * U + j
                    pe.wait_ge(max_in, s + 1)
                    pe.wait_ge(last_made, s + 1)
                    for g in range(G):
                        last = pe.matmul(nodeM[j % 2], onehot_last[:, j % 4, g, :], max_one[:, j % D, g, :],
                                         start=(g == 0), stop=(g == G - 1))
                    last.then_inc(node_max, 1)

                def to_nodes(t, j, _):
                    s = t * U + j
                    pe.wait_ge(rows_used, s + U + 1)
                    for g in range(G):
                        last = pe.matmul(total[j % 2], onehot[:, j, g, :],
                                         weighted[:, j % 2, g * HEADS:(g + 1) * HEADS, :].rearrange("p h w -> p (h w)"),
                                         start=(g == 0), stop=(g == G - 1))
                    last.then_inc(total_ready, 1)

                run_steps(pe, [(turn_hots, 0), (turn_scores, 0), (turn_back, 1), (to_edges, 2), (maxima, 1), (to_nodes, 4)], plan=DEEP)

            @block.scalar
            def _(act):
                act.sem_inc(hot_copied, 1)
                act.wait_ge(last_set, 16)
                act.wait_ge(flags, 2)

                def last_hots(t, j, _):
                    s = t * U + j
                    act.wait_ge(hot3, s + 1)
                    for g in range(G):
                        last = act.activation(onehot_last[:, j % 4, g, :], onehot[:, j, g, :], ACT.Copy, scale=last_flag[:, g, bass.ds(s, 1)])
                    last.then_inc(last_made, 1)

                def copy_hots(t, j, _):
                    s = t * U + j
                    act.wait_ge(hot_turned, s + 1)
                    act.activation(onehot_t[:, j % 4, :, :], hotT.rearrange("p (g n) -> p g n", g=G), ACT.Copy).then_inc(hot_copied, 1)

                def copy_maxima(t, j, _):
                    s = t * U + j
                    act.wait_ge(max_back, s + 1)
                    act.activation(max_one[:, j % D, :, 0:HEADS], maxT.rearrange("p (g h) -> p g h", g=G), ACT.Copy).then_inc(max_in, 1)

                def rescale(t, j, _):
                    s = t * U + j
                    act.wait_ge(dropped, s + 1)
                    act.activation(alpha[:, j % D, :], m_drop[:, j % D, :], ACT.Exp).then_inc(alpha_made, 1)

                def weights(t, j, _):
                    s = t * U + j
                    act.wait_ge(e_ready, s + 2)
                    act.activation(weight[:, j % D, :], e_diff[:, j % D, :], ACT.Exp).then_inc(weights_made, 1)

                for j in range(AHEAD):
                    place_indices(act, DEEP, src_idx, 0, j, rows_used, idx3, slot_free)

                def indices(t, j, _):
                    place_indices(act, DEEP, src_idx, t + (j + AHEAD) // U, (j + AHEAD) % U, rows_used, idx3, slot_free)

                run_steps(act, [(indices, 0), (last_hots, 0), (copy_hots, 0), (copy_maxima, 1), (rescale, 2), (weights, 3)], plan=DEEP)

            @block.vector
            def _(dve):
                dve.sem_inc(rows_used, U)
                dve.sem_inc(scan3, D)
                dve.sem_inc(e_ready, 1)
                dve.sem_inc(table_kept, 1)
                dve.sem_inc(added, 1)
                dve.memset(ones_row[0:1, :], 1.0).then_inc(flags, 1)
                dve.memset(max_one[:, :, :, HEADS:HEADS + 1], 1.0).then_inc(flags, 1)
                dve.memset(acc3, 0.0).then_inc(flags, 1)
                dve.memset(scan_buf[0:HEADS, 1, W - 1:W], 0.0).then_inc(flags, 1)
                dve.wait_ge(flags, 4)

                def by_head(v, j):
                    return v[:, j % D, :].rearrange("p (g h) -> p g h", g=G)

                def row(tile, part):
                    return node_tab[:, bass.ds(tile, 1), part].rearrange("p a k -> p (a k)")

                def scores(t, j, _):
                    s = t * U + j
                    dve.wait_ge(got3[j], 16 * G * (t + 1))
                    dve.tensor_tensor(by_head(src_score, j),
                                      edge_buf[:, j, :, :].rearrange("p g (h w) -> p g h w", w=HW + 1)[:, :, :, HW],
                                      score_e[:, :, :, bass.ds(s, 1)].rearrange("p h g a -> p g (h a)"), ALU.add).then_inc(scored, 1)

                def one_hots(t, j, _):
                    s = t * U + j
                    dve.tensor_tensor(onehot[:, j, :, :], iota_n[:, :].rearrange("p (a n) -> p a n", a=1).broadcast_to([P, G, P]),
                                      node_key[:, :, bass.ds(s, 1)].broadcast_to([P, G, P]), ALU.is_equal).then_inc(hot3, 1)

                def scan(t, j, _):
                    s = t * U + j
                    dve.wait_ge(score_turned, s + 1)
                    dve.wait_ge(pen3_in[j % D], 16 * ((t * (U // D) + j // D) + 1))
                    dve.wait_ge(scan3, s + D)
                    dve.tensor_tensor_scan(scan_buf[0:HEADS, j % 2, :], pen_buf[0:HEADS, j % D, :], scoreT,
                                           scan_buf[0:HEADS, (j - 1) % 2, W - 1:W], ALU.add, ALU.max).then_inc(scan3, 1)

                def mark_absent(t, j, _):
                    s = t * U + j
                    dve.wait_ge(node_max, s + 1)
                    dve.tensor_scalar(absent[:, j % D, :], nodeM[j % 2][:, HEADS:HEADS + 1], -1.0, 1.0, ALU.mult, ALU.add).then_inc(absent_made, 1)

                def fetch_target(t, j, tile):
                    dve.tensor_scalar(node_now[:, j % D, TARGET], row(tile, TARGET), 1.0, None, ALU.mult).then_inc(target_in, 1)

                def raise_src_top(t, j, tile):
                    s = t * U + j
                    dve.wait_ge(absent_made, s + 1)
                    dve.wait_ge(table_kept, s + 1)
                    dve.scalar_tensor_tensor(out=node_now[:, j % D, SRC_TOP], in0=row(tile, SRC_TOP), scalar=absent[:, j % D, :],
                                             in1=nodeM[j % 2][:, 0:HEADS], op0=ALU.mult, op1=ALU.add).then_inc(src_top, 1)

                def add_target(t, j, _):
                    s = t * U + j
                    dve.wait_ge(target_in, s + 1)
                    dve.wait_ge(src_top, s + 1)
                    dve.tensor_tensor(m_sum[:, j % D, :], node_now[:, j % D, SRC_TOP], node_now[:, j % D, TARGET], ALU.add).then_inc(sum_made, 1)

                def relu_top(t, j, _):
                    s = t * U + j
                    dve.wait_ge(sum_made, s + 1)
                    dve.scalar_tensor_tensor(out=node_now[:, j % D, TOP], in0=m_sum[:, j % D, :], scalar=0.2, in1=m_sum[:, j % D, :],
                                             op0=ALU.mult, op1=ALU.max).then_inc(top_made, 1)

                def drop(t, j, tile):
                    s = t * U + j
                    dve.wait_ge(top_made, s + 1)
                    dve.tensor_tensor(m_drop[:, j % D, :], row(tile, TOP), node_now[:, j % D, TOP], ALU.subtract).then_inc(dropped, 1)

                def keep(t, j, tile):
                    s = t * U + j
                    dve.wait_ge(dropped, s + 1)
                    both = slice(TOP.start, SRC_TOP.stop)
                    dve.tensor_scalar(row(tile, both), node_now[:, j % D, both], 1.0, None, ALU.mult).then_inc(table_kept, 1)

                def edge_scores(t, j, _):
                    s = t * U + j
                    dve.wait_ge(edge_values, s + 1)
                    dve.tensor_tensor(by_head(e_sum, j), by_head(src_score, j), edgeV[:, :, TARGET], ALU.add).then_inc(e_sum_made, 1)

                def relu_scores(t, j, _):
                    s = t * U + j
                    dve.wait_ge(e_sum_made, s + 1)
                    dve.scalar_tensor_tensor(out=e_relu[:, j % D, :], in0=e_sum[:, j % D, :], scalar=0.2, in1=e_sum[:, j % D, :],
                                             op0=ALU.mult, op1=ALU.max).then_inc(e_relu_made, 1)

                def less_top(t, j, _):
                    s = t * U + j
                    dve.wait_ge(e_relu_made, s + 1)
                    dve.tensor_tensor(by_head(e_diff, j), by_head(e_relu, j), edgeV[:, :, TOP], ALU.subtract).then_inc(e_ready, 1)

                def weigh(t, j, _):
                    s = t * U + j
                    dve.wait_ge(weights_made, s + 1)
                    dve.scalar_tensor_tensor(out=weighted[:, j % 2, :, :],
                                             in0=weight[:, j % D, :].rearrange("p (k a) -> p k a", a=1).broadcast_to([P, GH, HW]),
                                             scalar=1.0, in1=rows3[:, j, :, 0:HW], op0=ALU.min, op1=ALU.mult).then_inc(rows_used, 1)

                def sums(tile):
                    return acc3[:, bass.ds(tile, 1), :, :].rearrange("p a h w -> p (a h) w")

                def rescale_sums(t, j, tile):
                    s = t * U + j
                    dve.wait_ge(alpha_made, s + 1)
                    dve.wait_ge(added, s + 1)
                    dve.scalar_tensor_tensor(out=sums(tile), in0=alpha[:, j % D, :].rearrange("p (h a) -> p h a", a=1).broadcast_to([P, HEADS, HW]),
                                             scalar=1.0, in1=sums(tile), op0=ALU.min, op1=ALU.mult).then_inc(rescaled, 1)

                def add(t, j, tile):
                    s = t * U + j
                    dve.wait_ge(rescaled, s + 1)
                    dve.wait_ge(total_ready, s + 1)
                    dve.tensor_tensor(sums(tile), sums(tile), total[j % 2].rearrange("p (h w) -> p h w", h=HEADS), ALU.add).then_inc(added, 1)

                run_steps(dve, [(one_hots, 0), (scores, 0), (mark_absent, 2), (fetch_target, 2), (scan, 1), (raise_src_top, 2),
                                (edge_scores, 3), (add_target, 2), (relu_scores, 3), (relu_top, 2), (less_top, 3), (drop, 2),
                                (rescale_sums, 5), (keep, 2), (weigh, 4), (add, 5)],
                          before=lambda t: tiles_of_steps(t, [2, 5], U=U), plan=DEEP)

        f_chain, f_out = sem("final_chain"), sem("final_out")
        inv = stats[:, :, 0:HEADS]
        with nc.Block() as block:
            @block.vector
            def _(dve):
                step = Count(f_chain)

                def link(ins):
                    dve.wait_ge(f_chain, step.inc(ins))

                link(dve.tensor_scalar(inv, acc3[:, :, :, HO], 1e-10, None, ALU.add))
                link(dve.reciprocal(inv, inv))
                half = NT // 2
                for a, b in ((0, half), (half, NT)):
                    xs = x_sb[:, a:b, :].rearrange("p t (h o) -> p t h o", h=HEADS)
                    hs = h_sb[:, a:b, :].rearrange("p t (h o) -> p t h o", h=HEADS)
                    link(dve.tensor_tensor(hs, acc3[:, a:b, :, 0:HO],
                                           inv[:, a:b, :].rearrange("p t (h a) -> p t h a", a=1).broadcast_to([P, b - a, HEADS, HO]), ALU.mult))
                    link(dve.tensor_tensor(xs, xs, hs, ALU.add))

            @block.sync
            def _(sp):
                half = NT // 2
                sp.wait_ge(f_chain, 4)
                sp.dma_start(out[0:half * P, :].rearrange("(t p) f -> p t f", p=P), x_sb[:, 0:half, :]).then_inc(f_out, 16)
                sp.wait_ge(f_chain, 6)
                sp.dma_start(out[half * P:(NT - 1) * P, :].rearrange("(t p) f -> p t f", p=P), x_sb[:, half:NT - 1, :]).then_inc(f_out, 16)
                sp.dma_start(out[(NT - 1) * P:N, :], x_sb[0:LAST, NT - 1, :]).then_inc(f_out, 16)
                sp.wait_ge(f_out, 48)


_INS = ['x', 'src', 'dst', 'edge_attr_128', 'edge_attr_8', 'L0_gnn_u', 'L0_gnn_W1', 'L0_gnn_b1', 'L0_gnn_W2', 'L0_gnn_b2',
        'L1_gnn_W_l', 'L1_gnn_b_l', 'L1_gnn_W_r', 'L1_gnn_gn_weight', 'L1_gnn_gn_bias', 'L1_gnn_gn_mean_scale',
        'L2_gnn_W', 'L2_gnn_b', 'L3_gnn_W', 'L3_gnn_a']
_OUTS = [((6250, 128), 'float32')]


def kernel(**inputs):
    import numpy as _np
    import concourse.bacc as _bacc
    from concourse import mybir as _mybir
    from concourse.bass_utils import run_bass_kernel_spmd as _run

    nc = _bacc.Bacc("TRN2", target_bir_lowering=False, num_devices=1)
    arrays, args = {}, []
    for name in _INS:
        a = _np.ascontiguousarray(inputs[name])
        arrays[f"in_{name}_dram"] = a
        args.append(nc.dram_tensor(f"in_{name}_dram", a.shape, _mybir.dt.from_np(a.dtype), kind="ExternalInput").ap())
    for i, (shape, dtype) in enumerate(_OUTS):
        dt = _mybir.dt.from_np(_np.dtype(dtype))
        args.append(nc.dram_tensor(f"out_{i}_dram", shape, dt, kind="ExternalOutput").ap())
    gnn_program(nc, *args)
    r = _run(nc, [arrays], core_ids=[0])
    got = tuple(r.results[0][f"out_{i}_dram"] for i in range(len(_OUTS)))
    return got[0]
```
